# Optimizing a Trainium2 kernel written in Bass

```python
import numpy as np
import jax
import jax.numpy as jnp

def _softmax(x, axis=-1):
    return jax.nn.softmax(x, axis=axis)

def _gelu(x):
    return jax.nn.gelu(x, approximate=True)

def _silu(x):
    return jax.nn.silu(x)

def _sigmoid(x):
    return jax.nn.sigmoid(x)

def _layernorm(x, axis=-1, eps=1e-05):
    m = jnp.mean(x, axis=axis, keepdims=True)
    v = jnp.var(x, axis=axis, keepdims=True)
    return (x - m) / jnp.sqrt(v + eps)

def _scatter_add(tgt, idx, src, axis=0):
    return tgt.at[idx].add(src)

def _segment_sum(src, seg, n):
    return jax.ops.segment_sum(src, seg, n)
kernel_name = 'mk_seq_postln_d1_jaxref_r4_4f130a'

def setup_inputs(seed: int=0):
    np.random.seed(seed)
    _w = jnp.asarray

    def _L0_attn_setup():
        import jax, jax.numpy as jnp
        import numpy as np
        DIM = 1024
        N_HEADS = 32
        N_KV_HEADS = 8
        HEAD_DIM = DIM // N_HEADS
        N_REP = N_HEADS // N_KV_HEADS
        THETA = 10000.0
        B, S = (4, 256)

        def _rope_cos_sin(seq_len):
            freqs = 1.0 / THETA ** (jnp.arange(0, HEAD_DIM, 2, dtype=jnp.float32) / HEAD_DIM)
            t = jnp.arange(seq_len, dtype=jnp.float32)
            ang = jnp.outer(t, freqs)
            return (jnp.cos(ang), jnp.sin(ang))

        def _apply_rope(x, cos, sin):
            xr = x[..., 0::2]
            xi = x[..., 1::2]
            c = cos[None, :, None, :]
            s = sin[None, :, None, :]
            out_r = xr * c - xi * s
            out_i = xr * s + xi * c
            return jnp.stack([out_r, out_i], axis=-1).reshape(x.shape)
        key = jax.random.key(seed)
        ks = jax.random.split(key, 5)
        sc = 1.0 / np.sqrt(DIM).astype(np.float32)
        x = jax.random.normal(ks[0], (B, S, DIM), jnp.float32)
        wq = jax.random.normal(ks[1], (DIM, N_HEADS * HEAD_DIM), jnp.float32) * sc
        wk = jax.random.normal(ks[2], (DIM, N_KV_HEADS * HEAD_DIM), jnp.float32) * sc
        wv = jax.random.normal(ks[3], (DIM, N_KV_HEADS * HEAD_DIM), jnp.float32) * sc
        wo = jax.random.normal(ks[4], (N_HEADS * HEAD_DIM, DIM), jnp.float32) * sc
        return {'x': x, 'wq': wq, 'wk': wk, 'wv': wv, 'wo': wo}
    _L0_attn_in = _L0_attn_setup()

    def _L0_ffn_setup():
        import jax, jax.numpy as jnp
        import numpy as np
        H, FF = (1024, 3584)
        B, S = (4, 512)
        key = jax.random.key(seed)
        ks = jax.random.split(key, 7)
        x = jax.random.normal(ks[0], (B, S, H), dtype=jnp.float32)
        gate_t = jax.random.randint(ks[1], (FF, H), -1, 2, dtype=jnp.int32)
        up_t = jax.random.randint(ks[2], (FF, H), -1, 2, dtype=jnp.int32)
        down_t = jax.random.randint(ks[3], (H, FF), -1, 2, dtype=jnp.int32)
        gate_s = jax.random.uniform(ks[4], (FF,), jnp.float32, 0.01, 0.1)
        up_s = jax.random.uniform(ks[5], (FF,), jnp.float32, 0.01, 0.1)
        down_s = jax.random.uniform(ks[6], (H,), jnp.float32, 0.01, 0.1)
        return {'x': x, 'gate_t': gate_t, 'up_t': up_t, 'down_t': down_t, 'gate_s': gate_s, 'up_s': up_s, 'down_s': down_s}
    _L0_ffn_in = _L0_ffn_setup()
    _d = {'L0_attn_x': _L0_attn_in['x'], 'L0_attn_wq': _L0_attn_in['wq'], 'L0_attn_wk': _L0_attn_in['wk'], 'L0_attn_wv': _L0_attn_in['wv'], 'L0_attn_wo': _L0_attn_in['wo'], 'L0_ffn_gate_t': _L0_ffn_in['gate_t'], 'L0_ffn_up_t': _L0_ffn_in['up_t'], 'L0_ffn_down_t': _L0_ffn_in['down_t'], 'L0_ffn_gate_s': _L0_ffn_in['gate_s'], 'L0_ffn_up_s': _L0_ffn_in['up_s'], 'L0_ffn_down_s': _L0_ffn_in['down_s']}
    _x0 = _d['L0_attn_x']
    _d['L0_attn_x'] = jax.random.normal(jax.random.fold_in(jax.random.key(seed), 1), (4, 512, 1024), dtype=_x0.dtype)
    del _x0
    return _d

def reference(L0_attn_x, L0_attn_wq, L0_attn_wk, L0_attn_wv, L0_attn_wo, L0_ffn_gate_t, L0_ffn_up_t, L0_ffn_down_t, L0_ffn_gate_s, L0_ffn_up_s, L0_ffn_down_s):

    def _L0_attn_ref(x, wq, wk, wv, wo):
        import jax, jax.numpy as jnp
        import numpy as np
        DIM = 1024
        N_HEADS = 32
        N_KV_HEADS = 8
        HEAD_DIM = DIM // N_HEADS
        N_REP = N_HEADS // N_KV_HEADS
        THETA = 10000.0
        B, S = (4, 256)

        def _rope_cos_sin(seq_len):
            freqs = 1.0 / THETA ** (jnp.arange(0, HEAD_DIM, 2, dtype=jnp.float32) / HEAD_DIM)
            t = jnp.arange(seq_len, dtype=jnp.float32)
            ang = jnp.outer(t, freqs)
            return (jnp.cos(ang), jnp.sin(ang))

        def _apply_rope(x, cos, sin):
            xr = x[..., 0::2]
            xi = x[..., 1::2]
            c = cos[None, :, None, :]
            s = sin[None, :, None, :]
            out_r = xr * c - xi * s
            out_i = xr * s + xi * c
            return jnp.stack([out_r, out_i], axis=-1).reshape(x.shape)
        bsz, seq_len, _ = x.shape
        q = (x @ wq).reshape(bsz, seq_len, N_HEADS, HEAD_DIM)
        k = (x @ wk).reshape(bsz, seq_len, N_KV_HEADS, HEAD_DIM)
        v = (x @ wv).reshape(bsz, seq_len, N_KV_HEADS, HEAD_DIM)
        cos, sin = _rope_cos_sin(seq_len)
        q = _apply_rope(q, cos, sin)
        k = _apply_rope(k, cos, sin)
        k = jnp.repeat(k, N_REP, axis=2)
        v = jnp.repeat(v, N_REP, axis=2)
        scores = jnp.einsum('bqhd,bkhd->bhqk', q, k) / np.float32(np.sqrt(HEAD_DIM))
        mask = jnp.triu(jnp.full((seq_len, seq_len), -jnp.inf, dtype=scores.dtype), k=1)
        scores = scores + mask
        attn = jax.nn.softmax(scores.astype(jnp.float32), axis=-1).astype(q.dtype)
        out = jnp.einsum('bhqk,bkhd->bqhd', attn, v).reshape(bsz, seq_len, N_HEADS * HEAD_DIM)
        return out @ wo

    def _L0_ffn_ref(x, gate_t, up_t, down_t, gate_s, up_s, down_s):
        import jax, jax.numpy as jnp
        import numpy as np
        H, FF = (1024, 3584)
        B, S = (4, 512)
        Bb, Ss, Hh = x.shape
        x_flat = x.reshape(Bb * Ss, Hh)
        gate_w = gate_t.astype(jnp.float32) * gate_s[:, None]
        up_w = up_t.astype(jnp.float32) * up_s[:, None]
        down_w = down_t.astype(jnp.float32) * down_s[:, None]
        gate_out = x_flat @ gate_w.T
        up_out = x_flat @ up_w.T
        hidden = jax.nn.silu(gate_out) * up_out
        out_flat = hidden @ down_w.T
        return out_flat.reshape(Bb, Ss, -1)
    x = L0_attn_x
    x = _layernorm(x + _L0_attn_ref(x, L0_attn_wq, L0_attn_wk, L0_attn_wv, L0_attn_wo), axis=-1)
    x = _layernorm(x + _L0_ffn_ref(x, L0_ffn_gate_t, L0_ffn_up_t, L0_ffn_down_t, L0_ffn_gate_s, L0_ffn_up_s, L0_ffn_down_s), axis=-1)
    return x

_drawn_inputs = setup_inputs


def setup_inputs(seed=0):
    import zlib

    import numpy as np

    out = dict(_drawn_inputs(seed))
    spreads = {}
    factors = {}
    for name, (base, spread) in spreads.items():
        noise = np.random.default_rng([zlib.crc32(name.encode()), seed]).standard_normal(out[name].shape)
        drawn = base * np.exp(spread * noise) if base else spread * noise
        out[name] = jnp.asarray(drawn.astype(out[name].dtype))
    for name, factor in factors.items():
        out[name] = (out[name] * factor).astype(out[name].dtype)
    return out
```

```python
from contextlib import ExitStack

import numpy as np
import concourse.bass as bass
from concourse import mybir
from concourse.alu_op_type import AluOpType as ALU

F32, F16, BF16, I32 = mybir.dt.float32, mybir.dt.float16, mybir.dt.bfloat16, mybir.dt.int32
ACT = mybir.ActivationFunctionType

P = 128
B, S, D = 4, 512, 1024
NH, NKV, HD = 32, 8, 32
REP = NH // NKV
FF = 3584
KD = D // P
NT = S // P
TILES = B * NT
HALF = 512
UH = 8
UNITS = NH // UH
UG = UH // REP
FC = FF // P
GC = 4
EPS = 1e-5
THETA = 10000.0

STK = 3 * HD
STKM = STK + 2

X_UP, W_UP = 2.0 ** 6, 2.0 ** 8
PROJ_DOWN = 1.0 / (X_UP * W_UP)
QK_UP = 2.0 ** 4
V_UP = 2.0 ** 4
ATT_UP = 2.0 ** 6
OUT_DOWN = 1.0 / (ATT_UP * W_UP)
SCORE_DOWN = 1.0 / QK_UP ** 2
MAX_ONE = QK_UP ** 2
P_LOG_UP = 10 * float(np.log(2.0))
X1_UP = 2.0 ** 10
HID_BOUND = float(D) ** 2 / 2.0 ** 15
MASKED = -1.0e30


class Event:

    def __init__(self, sem):
        self.sem, self.count = sem, 0


class Queue:

    def __init__(self):
        self.todo, self.seen = [], {}

    def wait(self, *tickets):
        for t in tickets:
            if t is None:
                continue
            event, count = t
            if self.seen.get(id(event), 0) < count:
                self.seen[id(event)] = count
                self.todo.append(lambda e, s=event.sem, c=count: e.wait_ge(s, c))

    def do(self, make, event=None, by=1):
        if event is None:
            self.todo.append(lambda e, m=make: m(e))
            return None
        event.count += by
        self.todo.append(lambda e, m=make, s=event.sem, n=by: m(e).then_inc(s, n))
        return event, event.count

    def run(self, e):
        for step in self.todo:
            step(e)


def side_by_side(main, side, main_steps, side_steps):
    done = 0.0
    side_left = True
    for _ in main:
        done += side_steps / main_steps
        while side_left and done >= 1:
            done -= 1
            side_left = next(side, None) is not None
        yield True
    for _ in side:
        yield True


def block_kernel(nc, xT, x, wq, wkv, wo, gateT, upT, downT, gate_s, up_s, down_s,
                 rope, causal, causalT, identB, identH, out):
    x1_dram = nc.dram_tensor("x1_spill", [TILES, P, D], F32, kind="Internal").ap()
    x1T_dram = nc.dram_tensor("x1T_spill", [TILES, P, 2 * KD * P], F16, kind="Internal").ap()

    ctx = ExitStack()
    with ctx:
        pe, act, dve, pool, sp = (Queue() for _ in range(5))

        def ev(name):
            return Event(ctx.enter_context(nc.semaphore(name)))

        def psum(name, dt=F32, cols=HALF):
            return ctx.enter_context(nc.psum_tensor(name, [P, cols], dt))

        def sb(where, name, shape, dt):
            return where.enter_context(nc.sbuf_tensor(name, [P, *shape], dt))

        bank = [psum(f"bank{i}") for i in range(8)]

        KEPT = 4
        page = [sb(ctx, f"page{i}", [D], F32) for i in range(KEPT)]
        idH = sb(ctx, "idH", [P], F16)
        stats = sb(ctx, "stats", [2, 2, 6], F32)
        mv = sb(ctx, "mv", [2, 2], F32)
        rstd = sb(ctx, "rstd", [2, 3], F32)

        NPAGE = 6
        A = ctx.enter_context(ExitStack())
        page += [sb(A, f"page{i}", [D], F32) for i in range(KEPT, NPAGE)]
        page_ev = [ev(f"page{i}_dma") for i in range(NPAGE)]
        free_pages = [(i, ()) for i in range(NPAGE)]

        def take_page():
            return free_pages.pop(0)

        def give_page(i, *tickets):
            free_pages.append((i, tickets))

        def load(dst, src, event, queue=None, waits=()):
            q = queue or sp
            q.wait(*waits)
            return q.do(lambda e: e.dma_start(dst, src), event, 16)

        def load_page(src, view):
            i, before = take_page()
            return i, load(view(page[i]), src, page_ev[i], waits=before)

        e_ln = ev("ln_step")
        ln_last = [(), ()]

        def layernorm(row, slot, ready):
            dve.wait(ready, *ln_last[slot])
            for h in range(2):
                t = dve.do(lambda e, h=h: nc.vector.bn_stats(stats[:, slot, h, :], row[:, h * HALF:(h + 1) * HALF]), e_ln)
            dve.wait(t)
            t = dve.do(lambda e: nc.vector.bn_aggr(mv[:, slot, :], stats[:, slot, :, :]), e_ln)
            dve.wait(t)
            v, r, w = rstd[:, slot, 0:1], rstd[:, slot, 1:2], rstd[:, slot, 2:3]
            t = dve.do(lambda e: nc.vector.tensor_scalar(v, mv[:, slot, 1:2], EPS, None, ALU.add), e_ln)
            dve.wait(t)
            t = dve.do(lambda e: nc.vector.tensor_scalar(w.bitcast(I32), v.bitcast(I32), 1, None,
                                                         ALU.logical_shift_right), e_ln)
            dve.wait(t)
            t = dve.do(lambda e: nc.vector.tensor_scalar(r.bitcast(I32), w.bitcast(I32), -1.0, float(0x5F3759DF),
                                                         ALU.mult, ALU.add), e_ln)
            for _ in range(4):
                dve.wait(t)
                t = dve.do(lambda e: nc.vector.scalar_tensor_tensor(w, v, r, r, ALU.mult, ALU.mult), e_ln)
                dve.wait(t)
                t = dve.do(lambda e: nc.vector.tensor_scalar(w, w, -0.5, 1.5, ALU.mult, ALU.add), e_ln)
                dve.wait(t)
                t = dve.do(lambda e: nc.vector.tensor_tensor(r, r, w, ALU.mult), e_ln)
            dve.wait(t)
            t = dve.do(lambda e: nc.vector.tensor_scalar(row, row, mv[:, slot, 0:1], r,
                                                         ALU.subtract, ALU.mult), e_ln)
            ln_last[slot] = (t,)
            return t

        wq_p = sb(A, "wq_parts", [2, KD, D], F16)
        wkv_p = sb(A, "wkv_parts", [2, KD, 2 * NKV * HD], F16)
        wo_p = sb(A, "wo_parts", [2, KD, D], F16)
        xT_p = sb(A, "xT_parts", [2, KD, S], F16)
        qT = sb(A, "q_stack", [2, UH, S], F16)
        kT = sb(A, "k_stack", [2, NKV, S], F16)
        v_p = sb(A, "v_parts", [2, 2, NT, NKV * HD], F16)
        nat = sb(A, "stack_rows", [2, UH, STK], F16)
        ropeA = sb(A, "rope_cos", [2, UH * HD], F32)
        ropeB = sb(A, "rope_sin", [2, UH * HD], F32)
        NP32, NPP = 2, 7
        p32 = sb(A, "p32", [NP32, S], F32)
        p_p = sb(A, "p_parts", [NPP, 2, S], F16)
        att = sb(A, "att_parts", [2, KD, S], F16)
        tab = sb(A, "rope_tab", [NT, 4, HD], F32)
        cmask = sb(A, "cmask", [S], BF16)
        cmaskT = sb(A, "cmaskT", [P], BF16)
        idB = sb(A, "idB", [P], BF16)
        ones = sb(A, "ones", [HD], F16)
        exp_bias = sb(A, "exp_bias", [1], F32)
        mx = sb(A, "row_max", [2, NT, UH], F32)
        mneg = sb(A, "neg_max", [NT, UH], F32)
        m_p = sb(A, "max_parts", [NT, 2, UH], F16)
        mT = sb(A, "max_rows", [S], F16)

        e_const, e_const2 = ev("const_dma"), ev("const_set")
        consts = None
        for dst, src in ((idH[:, :], identH), (idB[:, :], identB), (cmask[:, :], causal), (cmaskT[:, :], causalT),
                         (tab[:, :, :, :], rope)):
            consts = load(dst, src, e_const, act)
        pool.wait(pool.do(lambda e: nc.gpsimd.memset(ones[:, :], 1.0), e_const2))
        pool.wait(pool.do(lambda e: nc.gpsimd.memset(exp_bias[:, :], P_LOG_UP), e_const2))
        const_set = pool.do(lambda e: nc.gpsimd.memset(kT[96:128, :, :, :], MAX_ONE), e_const2)

        e_hi, e_lo = ev("split_hi"), ev("split_lo")

        def split_page(i, arrived, n, hi, lo, up, before=()):
            src = page[i][:, 0:n]
            act.wait(arrived, *before)
            h = act.do(lambda e: nc.scalar.activation(hi, src, ACT.Copy, scale=up), e_hi)
            dve.wait(arrived, h, *before)
            l = dve.do(lambda e: nc.vector.scalar_tensor_tensor(lo, src, up, hi, ALU.mult, ALU.subtract), e_lo)
            give_page(i, h, l)
            return l

        def flat(ap):
            return ap.rearrange("p a b -> p (a b)")

        xT_ready = {}
        xT_free = [()]

        def load_x(b):
            before, xT_free[0] = xT_free[0], ()
            for k in range(0, KD, 2):
                while not free_pages:
                    yield True
                i, t = load_page(xT[b, :, k:k + 2, :], lambda pg: pg[:, :].rearrange("p (a b) -> p a b", a=2))
                xT_ready[b, k] = xT_ready[b, k + 1] = split_page(
                    i, t, D, flat(xT_p[:, 0, k:k + 2, :]), flat(xT_p[:, 1, k:k + 2, :]), X_UP, before)
                yield True

        wkv_ready, wq_ready, wo_ready = {}, {}, {}

        def load_wkv():
            for k in range(0, KD, 2):
                i, t = load_page(wkv[:, k:k + 2, :], lambda pg: pg[:, :].rearrange("p (a b) -> p a b", a=2))
                wkv_ready[k] = wkv_ready[k + 1] = split_page(
                    i, t, D, flat(wkv_p[:, 0, k:k + 2, :]), flat(wkv_p[:, 1, k:k + 2, :]), W_UP)

        def load_square(w, parts, ready):
            for k in range(KD):
                while not free_pages:
                    yield True
                i, t = load_page(w[:, k, :], lambda pg: pg[:, :])
                ready[k] = split_page(i, t, D, parts[:, 0, k, :], parts[:, 1, k, :], W_UP)
                yield True

        readers = {i: () for i in range(8)}
        PROJ, TRANS, SCORE, PV, DEN = (0, 1), (2,), (3, 4, 5), 6, 7
        turn = {PROJ: 0, SCORE: 0}

        def next_bank(ring):
            i = ring[turn[ring] % len(ring)]
            turn[ring] += 1
            return i

        e_proj, e_rope, e_ropep, e_nathi, e_natlo = ev("proj"), ev("rope"), ev("rope_sum"), ev("nat_hi"), ev("nat_lo")
        e_tr, e_trc = ev("transposed"), ev("stack_copied")
        nat_turn = [0]
        nat_readers = [(), ()]
        rope_readers = [(), ()]
        pool_last = [const_set]

        def three_passes(dst, lhs, rhs, ready):
            for k in range(KD):
                pe.wait(*ready(k))
                for n, (a, c) in enumerate(((0, 0), (0, 1), (1, 0))):
                    first, last = k == 0 and n == 0, k == KD - 1 and n == 2
                    t = pe.do(lambda e, left=lhs(a, k), right=rhs(c, k), first=first, last=last:
                              nc.tensor.matmul(dst, left, right, start=first, stop=last), e_proj if last else None)
            return t

        def rotate(bk, nh, t, kind, ready):
            s = nat_turn[0] % 2
            nat_turn[0] += 1
            src = bank[bk][:, 0:nh * HD].rearrange("p (h c) -> p h c", h=nh)
            ta = ropeA[:, s, 0:nh * HD].rearrange("p (h c) -> p h c", h=nh)
            tb = ropeB[:, s, 0:nh * HD].rearrange("p (h c) -> p h c", h=nh)
            q = HD // 2

            def tabled(n, lo, hi):
                return tab[:, t:t + 1, 2 * kind + n, lo:hi].broadcast_to([P, nh, hi - lo])

            dve.wait(ready, consts, *rope_readers[s])
            dve.do(lambda e: nc.vector.tensor_tensor(ta, src, tabled(0, 0, HD), ALU.mult))
            dve.do(lambda e: nc.vector.tensor_tensor(tb[:, :, 0:q], src[:, :, q:HD], tabled(1, 0, q), ALU.mult))
            r = dve.do(lambda e: nc.vector.tensor_tensor(tb[:, :, q:HD], src[:, :, 0:q], tabled(1, q, HD), ALU.mult), e_rope)
            readers[bk] = readers[bk] + (r,)
            pool.wait(r, pool_last[0])
            r = pool_last[0] = pool.do(lambda e: nc.gpsimd.tensor_tensor(ropeA[:, s, 0:nh * HD], ropeA[:, s, 0:nh * HD],
                                                          ropeB[:, s, 0:nh * HD], ALU.add), e_ropep)
            rows = nat[:, s, 0:nh, :].rearrange("p h (f c) -> p h f c", f=3)
            field = (slice(0, 3, 2), 1) if kind else (slice(0, 2), 2)
            act.wait(r, *nat_readers[s])
            h = act.do(lambda e: nc.scalar.activation(
                rows[:, :, field[0], :], ta.unsqueeze(2).broadcast_to([P, nh, 2, HD]), ACT.Copy), e_nathi)
            dve.wait(r, h)
            l = dve.do(lambda e: nc.vector.tensor_tensor(rows[:, :, field[1], :], ta, rows[:, :, 0, :], ALU.subtract), e_natlo)
            rope_readers[s] = (h, l)
            return s, l

        def transpose_heads(s, nh, ready, dst, before, consts_ready):
            tb = bank[TRANS[0]][:, :].bitcast(F16).rearrange("p (h c) -> p h c", h=8)
            pe.wait(ready, consts_ready, *readers[TRANS[0]])
            for h in range(nh):
                t = pe.do(lambda e, h=h: nc.tensor.transpose(tb[0:STK, h, :], nat[:, s, h, :], idH[:, :]),
                          e_tr if h == nh - 1 else None)
            nat_readers[s] = (t,)
            dve.wait(t, *before)
            c = dve.do(lambda e: nc.vector.tensor_copy(dst, tb[0:STK, 0:nh, :]), e_trc)
            readers[TRANS[0]] = (c,)
            return c

        k_ready, v_ready, q_ready = {}, {}, {}
        st_done = {}
        pv_done = {}
        e_vhi, e_vlo = ev("v_hi"), ev("v_lo")

        def project(u, with_kv):
            b = u // UNITS
            late = []
            jobs = ([("kv", t) for t in range(NT)] if with_kv else []) + [("q", t) for t in range(NT)]
            for n, (what, t) in enumerate(jobs):
                bk = next_bank(PROJ)
                pe.wait(*readers[bk])
                readers[bk] = ()
                rows = slice(t * P, (t + 1) * P)
                if what == "kv":
                    done = three_passes(bank[bk][:, :], lambda a, k: xT_p[:, a, k, rows],
                                        lambda c, k: wkv_p[:, c, k, :], lambda k: (xT_ready[b, k], wkv_ready[k]))
                    nk = NKV * HD
                    act.wait(done, *([pv_done.get((b - 1) * UNITS - 1)] if b >= 2 else []))
                    vh, vl = v_p[:, b % 2, 0, t, :], v_p[:, b % 2, 1, t, :]
                    h = act.do(lambda e, bk=bk, vh=vh: nc.scalar.activation(vh, bank[bk][:, nk:2 * nk], ACT.Copy,
                                                                  scale=PROJ_DOWN * V_UP), e_vhi)
                    dve.wait(done, h)
                    l = dve.do(lambda e, bk=bk, vh=vh, vl=vl: nc.vector.scalar_tensor_tensor(
                        vl, bank[bk][:, nk:2 * nk], PROJ_DOWN * V_UP, vh, ALU.mult, ALU.subtract), e_vlo)
                    v_ready[b, t] = l
                    readers[bk] = (h, l)
                    s, ready = rotate(bk, NKV, t, 1, done)
                    dst = kT[0:STK, b % 2, :, rows]
                    before = [st_done.get((b - 1) * UNITS - 1)] if b >= 2 else []
                    job = (s, NKV, ready, dst, before, k_ready, (b, t))
                else:
                    g = u % UNITS
                    done = three_passes(bank[bk][:, 0:UH * HD], lambda a, k: xT_p[:, a, k, rows],
                                        lambda c, k: wq_p[:, c, k, g * UH * HD:(g + 1) * UH * HD],
                                        lambda k: (xT_ready[b, k], wq_ready[k]))
                    s, ready = rotate(bk, UH, t, 0, done)
                    job = (s, UH, ready, qT[0:STK, u % 2, :, rows], [st_done.get(u - 2)], q_ready, (u, t))
                    if t == NT - 1 and g == UNITS - 1:
                        xT_free[0] = (done,)
                late.append(job)
                yield True
                if len(late) > 1:
                    s, nh, ready, dst, before, record, key = late.pop(0)
                    record[key] = transpose_heads(s, nh, ready, dst, before, consts)
            yield True
            for s, nh, ready, dst, before, record, key in late:
                record[key] = transpose_heads(s, nh, ready, dst, before, consts)
            yield True

        e_smax, e_mx, e_mpart, e_mtr, e_mcopy = ev("score_q"), ev("row_max"), ev("max_part"), ev("max_tr"), ev("max_copy")
        e_mrow = [ev("max_rows_dma0"), ev("max_rows_dma1")]
        m_ready = {}

        def maxima(u):
            b, g = divmod(u, UNITS)
            for i in range(NT):
                n = (i + 1) * P
                for h in range(UH):
                    kv = (g * UH + h) // REP
                    bk = next_bank(SCORE)
                    pe.wait(q_ready[u, i], k_ready[b, i], *readers[bk])
                    t = pe.do(lambda e, bk=bk, h=h, kv=kv, i=i, n=n: nc.tensor.matmul(
                        bank[bk][:, 0:n], qT[0:STK, u % 2, h, i * P:n], kT[0:STK, b % 2, kv, 0:n],
                        start=True, stop=True), e_smax)
                    dve.wait(t)
                    r = dve.do(lambda e, bk=bk, h=h, i=i, n=n: nc.vector.tensor_tensor_reduce(
                        out=bank[bk][:, 0:n], in0=bank[bk][:, 0:n], in1=cmask[:, S - n:S], scale=1.0, scalar=MASKED,
                        op0=ALU.add, op1=ALU.max, accum_out=mx[:, u % 2, i, h:h + 1]), e_mx)
                    readers[bk] = (r,)
                    if h % 2:
                        yield True
            dve.wait(r, m_ready.get(("tr", u - 1)))
            mm = mx[:, u % 2, :, :]
            a = dve.do(lambda e: nc.vector.tensor_scalar(mneg[:, :, :], mm, -1.0 / MAX_ONE, None, ALU.mult), e_mpart)
            dve.wait(a)
            a = dve.do(lambda e: nc.vector.tensor_copy(m_p[:, :, 0, :], mneg[:, :, :]), e_mpart)
            dve.wait(a)
            a = dve.do(lambda e: nc.vector.tensor_tensor(m_p[:, :, 1, :], mneg[:, :, :], m_p[:, :, 0, :], ALU.subtract), e_mpart)
            yield True
            tb = bank[TRANS[0]][:, :].bitcast(F16)
            pe.wait(a, *readers[TRANS[0]])
            for i in range(NT):
                t = pe.do(lambda e, i=i: nc.tensor.transpose(tb[0:2 * UH, i * P:(i + 1) * P],
                                                             m_p[:, i, :, :].rearrange("p a h -> p (a h)"), idH[:, :]),
                          e_mtr if i == NT - 1 else None)
            m_ready["tr", u] = t
            dve.wait(t, *m_ready.get(("dma", u - 1), ()))
            c = dve.do(lambda e: nc.vector.tensor_copy(mT[0:2 * UH, :], tb[0:2 * UH, 0:S]), e_mcopy)
            readers[TRANS[0]] = (c,)
            both = []
            for a in range(2):
                both.append(load(qT[STK + a:STK + a + 1, u % 2, :, :], mT[a * UH:(a + 1) * UH, :], e_mrow[a], sp,
                                 waits=(c, st_done.get(u - 2))))
            m_ready["dma", u] = tuple(both)
            m_ready[u] = tuple(both)
            yield True

        e_st, e_exp, e_phi, e_plo, e_pv = ev("score_k"), ev("exp"), ev("p_hi"), ev("p_lo"), ev("pv")
        e_rden, e_att, e_atthi, e_attlo = ev("rden"), ev("att"), ev("att_hi"), ev("att_lo")
        p32_readers, pp_readers = [()] * NP32, [()] * NPP
        p_turn = [0, 0]
        att_ready, att_free = {}, [()]
        rden_last = [()]

        def attend(u):
            b, g = divmod(u, UNITS)
            late = None

            def pv(G, j, slots, ready):
                lo = j * P
                pe.wait(v_ready[b, j], *ready)
                if j == 0:
                    pe.wait(*readers[PV], *readers[DEN])
                for dst, steps in ((PV, ((0, 0), (1, 0), (0, 1))), (DEN, ((None, 0), (None, 1)))):
                    for n, (vp, pp) in enumerate(steps):
                        for hh in range(REP):
                            lhs = ones[:, :] if vp is None else v_p[:, b % 2, vp, j, (g * UG + G) * HD:(g * UG + G + 1) * HD]
                            final = dst == DEN and n == 1 and hh == REP - 1
                            t = pe.do(lambda e, dst=dst, hh=hh, lhs=lhs, pp=pp, n=n, sl=slots[hh], steps=steps: nc.tensor.matmul(
                                bank[dst][hh * HD:(hh + 1) * HD, lo:S], lhs, p_p[:, sl, pp, lo:S],
                                start=(j == 0 and n == 0), stop=(j == NT - 1 and n == len(steps) - 1),
                                tile_position=(0, hh * HD)),
                                e_pv if final else None)
                for s in slots:
                    pp_readers[s] = (t,)
                pv_done[u] = t
                if j < NT - 1:
                    return
                gg = g * UG + G
                i, before = take_page()
                rd, at = page[i][:, 0:S], page[i][:, S:2 * S]
                dve.wait(t, *before)
                r = dve.do(lambda e: nc.vector.reciprocal(rd, bank[DEN][:, :]), e_rden)
                dve.wait(r)
                a = dve.do(lambda e: nc.vector.scalar_tensor_tensor(at, bank[PV][:, :], ATT_UP / V_UP, rd,
                                                                    ALU.mult, ALU.mult), e_att)
                readers[PV] = readers[DEN] = (a,)
                act.wait(a, *att_free[0])
                h = act.do(lambda e: nc.scalar.activation(att[:, 0, gg, :], at, ACT.Copy), e_atthi)
                dve.wait(h, *att_free[0])
                l = dve.do(lambda e: nc.vector.tensor_tensor(att[:, 1, gg, :], at, att[:, 0, gg, :], ALU.subtract), e_attlo)
                give_page(i, l)
                att_ready[b, gg] = l

            for G in range(UG):
                kv = g * UG + G
                for j in range(NT):
                    lo = j * P
                    slots, ready = [], []
                    for hh in range(REP):
                        h = G * REP + hh
                        bk = next_bank(SCORE)
                        pe.wait(*m_ready[u], const_set, *[q_ready[u, i] for i in range(j, NT)], k_ready[b, j], *readers[bk])
                        pe.do(lambda e, bk=bk, h=h, lo=lo, kv=kv: nc.tensor.matmul(
                            bank[bk][:, 0:S - lo], kT[0:STKM, b % 2, kv, lo:lo + P], qT[0:STKM, u % 2, h, lo:S],
                            start=True, stop=False))
                        t = pe.do(lambda e, bk=bk: nc.tensor.matmul(bank[bk][:, 0:P], idB[:, :], cmaskT[:, :],
                                                                    start=False, stop=True), e_st)
                        st_done[u] = t
                        a, c = p_turn[0] % NP32, p_turn[1] % NPP
                        p_turn[0] += 1
                        p_turn[1] += 1
                        act.wait(t, *p32_readers[a], const_set)
                        x_ = act.do(lambda e, bk=bk, a=a, lo=lo: nc.scalar.activation(
                            p32[:, a, lo:S], bank[bk][:, 0:S - lo], ACT.Exp, bias=exp_bias[:, :], scale=SCORE_DOWN), e_exp)
                        readers[bk] = (x_,)
                        act.wait(x_, *pp_readers[c])
                        hi = act.do(lambda e, a=a, c=c, lo=lo: nc.scalar.activation(
                            p_p[:, c, 0, lo:S], p32[:, a, lo:S], ACT.Copy), e_phi)
                        dve.wait(hi)
                        l = dve.do(lambda e, a=a, c=c, lo=lo: nc.vector.tensor_tensor(
                            p_p[:, c, 1, lo:S], p32[:, a, lo:S], p_p[:, c, 0, lo:S], ALU.subtract), e_plo)
                        p32_readers[a] = (l,)
                        slots.append(c)
                        ready.append(l)
                        if hh == 1 and late:
                            pv(*late)
                            late = None
                        yield True
                    late = (G, j, slots, ready)
            pv(*late)
            yield True

        e_res, e_x1hi, e_x1lo, e_x1tr, e_x1c = ev("residual"), ev("x1_hi"), ev("x1_lo"), ev("x1_tr"), ev("x1_copy")
        x1_stored, x1T_stored = {}, {}
        sent = []

        def output(b):
            late = []

            def transposed(tile, i, l):
                while not free_pages:
                    yield True
                o, before = take_page()
                parts = page[i][:, :].bitcast(F16).rearrange("p (a k c) -> p a k c", a=2, k=KD)
                dst = page[o][:, :].bitcast(F16).rearrange("p (a k c) -> p a k c", a=2, k=KD)
                tb = bank[TRANS[0]][:, :].bitcast(F16).rearrange("p (h c) -> p h c", h=KD)
                for a in range(2):
                    pe.wait(l, *readers[TRANS[0]])
                    for k in range(KD):
                        t = pe.do(lambda e, a=a, k=k: nc.tensor.transpose(tb[:, k, :], parts[:, a, k, :], idH[:, :]),
                                  e_x1tr if k == KD - 1 else None)
                    act.wait(t, *before)
                    c = act.do(lambda e, a=a: nc.scalar.activation(dst[:, a, :, :], tb[:, :, :], ACT.Copy), e_x1c)
                    readers[TRANS[0]] = (c,)
                    yield True
                give_page(i, t)
                s = load(x1T_dram[tile], page[o][:, :].bitcast(F16), page_ev[o], sp, waits=(c,))
                x1T_stored[tile] = s
                give_page(o, s)

            for t in range(NT):
                tile = b * NT + t
                while len(free_pages) < 2:
                    yield True
                i, arrived = load_page(x[tile], lambda pg: pg[:, :])
                row = page[i][:, :]
                for h in range(2):
                    cols = slice(h * HALF, (h + 1) * HALF)
                    bk = next_bank(PROJ)
                    pe.wait(*readers[bk])
                    done = three_passes(bank[bk][:, :], lambda a, k: att[:, a, k, t * P:(t + 1) * P],
                                        lambda c, k: wo_p[:, c, k, cols], lambda k: (att_ready[b, k], wo_ready[k]))
                    dve.wait(done, arrived)
                    r = dve.do(lambda e, bk=bk, cols=cols, i=i: nc.vector.scalar_tensor_tensor(
                        page[i][:, cols], bank[bk][:, :], OUT_DOWN, page[i][:, cols], ALU.mult, ALU.add), e_res)
                    readers[bk] = (r,)
                    yield True
                if t == NT - 1:
                    att_free[0] = (done,)
                n = layernorm(row, tile % 2, r)
                s = load(x1_dram[tile], row, page_ev[i], sp, waits=(n,))
                x1_stored[tile] = s
                while not free_pages:
                    yield True
                o, before = take_page()
                hi, lo = page[o][:, 0:HALF].bitcast(F16), page[o][:, HALF:D].bitcast(F16)
                act.wait(n, *before)
                h_ = act.do(lambda e, hi=hi, row=row: nc.scalar.activation(hi, row, ACT.Copy, scale=X1_UP), e_x1hi)
                dve.wait(h_, *before)
                l = dve.do(lambda e, hi=hi, lo=lo, row=row: nc.vector.scalar_tensor_tensor(
                    lo, row, X1_UP, hi, ALU.mult, ALU.subtract), e_x1lo)
                give_page(i, s, h_, l)
                late.append((tile, o, l))
                yield True
                if len(late) > 1:
                    yield from transposed(*late.pop(0))
            for j in late:
                yield from transposed(*j)

        NU = B * UNITS
        wq_load, wo_load = load_square(wq, wq_p, wq_ready), load_square(wo, wo_p, wo_ready)
        first = load_x(0)
        wkv_steps = load_wkv()
        next(first)
        for _ in first:
            pass
        for _ in wq_load:
            pass
        for _ in project(0, True):
            pass
        for _ in wo_load:
            pass
        for _ in maxima(0):
            pass

        def chain(*streams):
            for s in streams:
                yield from s

        for u in range(NU):
            b, g = divmod(u, UNITS)
            streams, steps = [], 0
            if g == 0 and b > 0:
                streams.append(output(b - 1))
                steps += 24
            if u + 1 < NU:
                if (u + 1) % UNITS == 0:
                    streams.append(load_x((u + 1) // UNITS))
                    steps += 4
                streams += [project(u + 1, (u + 1) % UNITS == 0), maxima(u + 1)]
                steps += 6 + 18 + (4 if (u + 1) % UNITS == 0 else 0)
            for _ in side_by_side(chain(*streams), attend(u), max(steps, 1), 28):
                pass
        for _ in output(B - 1):
            pass

        A.close()
        page_users = tuple(t for i, ts in free_pages if i >= KEPT for t in ts)
        free_pages[:] = [(i, ts) for i, ts in free_pages if i < KEPT]
        over = page_users + tuple((e, e.count) for e in (e_proj, e_trc, e_pv, e_st, e_attlo, e_plo, e_x1tr, e_x1c, e_x1lo, e_res,
                                            e_hi, e_lo, e_mx, e_mcopy, e_phi, e_natlo, e_vlo, e_ln, *e_mrow))

        BB = ctx.enter_context(ExitStack())
        x1T = sb(BB, "x1T", [TILES, 2, KD, P], F16)
        acc = sb(BB, "acc", [TILES, D], F32)
        hid = sb(BB, "hid", [2, GC, 2, S], F16)
        NW = 7
        w_gate = sb(BB, "w_gate", [NW, KD, P], F16)
        w_up = sb(BB, "w_up", [NW, KD, P], F16)
        w_down = sb(BB, "w_down", [NW, D], F16)
        silu = sb(BB, "silu", [2, S], F32)
        sg = sb(BB, "sg", [FC], F32)
        su = sb(BB, "su", [FC], F32)
        sc = sb(BB, "sc", [8], F32)
        sq = sb(BB, "sq", [1], F32)

        e_sc, e_sdma = ev("scales"), ev("scale_dma")
        act.wait(*over)
        load(sg[:, :], gate_s, e_sdma, act)
        s_in = load(su[:, :], up_s, e_sdma, act)
        RMAX = bass.bass_isa.ReduceOp.max
        dve.wait(s_in, *over)
        dve.do(lambda e: nc.vector.tensor_reduce(sc[:, 0:1], sg[:, :], mybir.AxisListType.X, ALU.max,
                                                 apply_absolute_value=True))
        t = dve.do(lambda e: nc.vector.tensor_reduce(sc[:, 1:2], su[:, :], mybir.AxisListType.X, ALU.max,
                                                     apply_absolute_value=True), e_sc)
        pool.wait(t, pool_last[0])
        t = pool.do(lambda e: nc.gpsimd.partition_all_reduce(sc[:, 2:4], sc[:, 0:2], P, RMAX), e_sc)
        dve.wait(t)
        t = dve.do(lambda e: nc.vector.tensor_scalar(sc[:, 4:5], sc[:, 2:3], sc[:, 3:4], HID_BOUND, ALU.mult, ALU.mult), e_sc)
        dve.wait(t)
        t = dve.do(lambda e: nc.vector.tensor_scalar(sc[:, 5:6], sc[:, 4:5], 1e-30, None, ALU.max), e_sc)
        dve.wait(t)
        t = dve.do(lambda e: nc.vector.reciprocal(sc[:, 6:7], sc[:, 5:6]), e_sc)
        dve.wait(t)
        dve.do(lambda e: nc.vector.tensor_scalar(sg[:, :], sg[:, :], 1.0 / X1_UP, None, ALU.mult))
        scales = dve.do(lambda e: nc.vector.tensor_scalar(su[:, :], su[:, :], sc[:, 6:7], 1.0 / X1_UP, ALU.mult, ALU.mult), e_sc)

        e_w = ev("weights_cast")
        w_ready = {}

        def weights(c, kinds, free):
            for kind in kinds:
                w, dst = ((gateT, w_gate), (upT, w_up), (downT, w_down))[kind]
                while not free_pages:
                    yield True
                i, before = take_page()
                pg = page[i][:, :].bitcast(I32)
                arrived = load(pg, w[c], page_ev[i], sp, waits=before)
                to = dst[:, c % NW, :] if kind == 2 else flat(dst[:, c % NW, :, :])
                act.wait(arrived, *free)
                t = act.do(lambda e, to=to, pg=pg: nc.scalar.activation(to, pg, ACT.Copy), e_w)
                give_page(i, t)
                w_ready[c, kind] = t
                yield True

        e_x1T = [ev(f"x1T_load{t}") for t in range(B)]
        x1T_ready = {}

        def load_x1T():
            for tb in range(B):
                for t in range(tb * NT, (tb + 1) * NT):
                    x1T_ready[tb] = load(x1T[:, t, :, :, :].rearrange("p a k c -> p (a k c)"), x1T_dram[t], e_x1T[tb], sp,
                                         waits=(x1T_stored[t], *over))

        GATE, UP, DOWN = (0, 1), (2, 3), (4, 5, 6, 7)
        breaders = {i: over for i in range(8)}
        for r in (GATE, UP, DOWN):
            turn[r] = 0
        e_gu, e_silu, e_h, e_hhi, e_hlo = ev("gate_up"), ev("silu"), ev("hidden"), ev("hid_hi"), ev("hid_lo")
        e_down, e_acc, e_fin = ev("down"), ev("acc"), ev("final")
        silu_readers, hid_readers = [over] * 2, [over] * 2
        small = [0]
        acc_ready = {}

        def gate_up(g, tb, slot, hid_ready):
            for c in range(GC):
                ch = g * GC + c
                w = ch % NW
                gb, ub = next_bank(GATE), next_bank(UP)
                for kind, bk, ws in ((0, gb, w_gate), (1, ub, w_up)):
                    pe.wait(w_ready[ch, kind], x1T_ready[tb], *breaders[bk])
                    for k in range(KD):
                        for a in range(2):
                            t = pe.do(lambda e, bk=bk, ws=ws, w=w, k=k, a=a: nc.tensor.matmul(
                                bank[bk][:, :], ws[:, w, k, :], x1T[:, tb * NT:(tb + 1) * NT, a, k, :],
                                start=(k == 0 and a == 0), stop=(k == KD - 1 and a == 1)),
                                e_gu if k == KD - 1 and a == 1 else None)
                    if kind == 0:
                        gt = t
                s = small[0] % 2
                small[0] += 1
                act.wait(gt, scales, *silu_readers[s])
                x_ = act.do(lambda e, gb=gb, ch=ch, s=s: nc.scalar.activation(silu[:, s, :], bank[gb][:, :], ACT.Silu,
                                                                              scale=sg[:, ch:ch + 1]), e_silu)
                breaders[gb] = (x_,)
                dve.wait(t, x_)
                h = dve.do(lambda e, ub=ub, ch=ch, s=s: nc.vector.scalar_tensor_tensor(
                    silu[:, s, :], bank[ub][:, :], su[:, ch:ch + 1], silu[:, s, :], ALU.mult, ALU.mult), e_h)
                breaders[ub] = (h,)
                act.wait(h, *hid_readers[slot])
                hi = act.do(lambda e, c=c, s=s: nc.scalar.activation(hid[:, slot, c, 0, :], silu[:, s, :], ACT.Copy), e_hhi)
                dve.wait(hi)
                l = dve.do(lambda e, c=c, s=s: nc.vector.tensor_tensor(hid[:, slot, c, 1, :], silu[:, s, :],
                                                                       hid[:, slot, c, 0, :], ALU.subtract), e_hlo)
                silu_readers[s] = (hi, l)
                hid_ready.append(l)
                yield True
            if tb == B - 1:
                gu_last[g] = t

        def down(g, tb, slot, hid_ready):
            last_group = g == FC // GC - 1
            for i in range(NT):
                tile = tb * NT + i
                for h in range(2):
                    cols = slice(h * HALF, (h + 1) * HALF)
                    bk = next_bank(DOWN)
                    pe.wait(*breaders[bk], *hid_ready)
                    for c in range(GC):
                        ch = g * GC + c
                        pe.wait(w_ready[ch, 2])
                        for a in range(2):
                            t = pe.do(lambda e, bk=bk, c=c, a=a, i=i, ch=ch, cols=cols: nc.tensor.matmul(
                                bank[bk][:, :], hid[:, slot, c, a, i * P:(i + 1) * P], w_down[:, ch % NW, cols],
                                start=(c == 0 and a == 0), stop=(c == GC - 1 and a == 1)),
                                e_down if c == GC - 1 and a == 1 else None)
                    dve.wait(t, *(over if g == 0 else acc_ready[tile, h]))
                    dst = acc[:, tile, cols]
                    if g == 0:
                        r = dve.do(lambda e, bk=bk, dst=dst: nc.vector.tensor_copy(dst, bank[bk][:, :]), e_acc)
                    else:
                        r = dve.do(lambda e, bk=bk, dst=dst: nc.vector.tensor_tensor(dst, bank[bk][:, :], dst, ALU.add), e_acc)
                    breaders[bk] = (r,)
                    acc_ready[tile, h] = (r,)
                if last_group:
                    yield from finish(tile, r)
                yield True
            hid_readers[slot] = (t,)
            if tb == B - 1:
                down_last[g] = t

        gu_last, down_last = {}, {}
        ds = [None]

        def finish(tile, r):
            if ds[0] is None:
                d, arrived = load_page(down_s.partition_broadcast(P), lambda pg: pg[:, :])
                dve.wait(arrived)
                t = dve.do(lambda e: nc.vector.tensor_scalar(page[d][:, :], page[d][:, :], sc[:, 5:6], None, ALU.mult), e_fin)
                ds[0] = (d, t)
            while not free_pages:
                yield True
            d, dt_ = ds[0]
            i, before = take_page()
            arrived = load(page[i][:, :], x1_dram[tile], page_ev[i], sp, waits=(x1_stored[tile], *before))
            row = acc[:, tile, :]
            dve.wait(r, dt_)
            t = dve.do(lambda e: nc.vector.tensor_tensor(row, row, page[d][:, :], ALU.mult), e_fin)
            dve.wait(t, arrived)
            t = dve.do(lambda e: nc.vector.tensor_tensor(row, row, page[i][:, :], ALU.add), e_fin)
            give_page(i, t)
            n = layernorm(row, tile % 2, t)
            sp.wait(n)
            sp.do(lambda e: e.dma_start(out[tile], row), e_out, 16)

        e_out = ev("out_dma")
        NG = FC // GC

        def group_weights(g, kinds, last):
            for c in range(g * GC, min((g + 1) * GC, FC)):
                free = over
                if c >= NW:
                    while (c - NW) // GC not in last:
                        yield True
                    free = (last[(c - NW) // GC],)
                yield from weights(c, kinds, free)

        def gate_up_weights(g):
            return group_weights(g, (0, 1), gu_last)

        def down_weights(g):
            return group_weights(g, (2,), down_last)

        def drain(stream):
            for _ in stream:
                pass

        first_w = gate_up_weights(0)
        for _ in range(3):
            next(first_w)
        load_x1T()
        drain(first_w)
        loads = down_weights(0)
        pending = None
        for g in range(NG):
            for tb in range(B):
                slot = (g * B + tb) % 2
                ready = []
                for _ in gate_up(g, tb, slot, ready):
                    next(loads, None)
                if pending:
                    if pending[1] == 0:
                        drain(loads)
                        loads = gate_up_weights(pending[0] + 1)
                    for _ in down(*pending):
                        next(loads, None)
                pending = (g, tb, slot, ready)
            drain(loads)
            loads = down_weights(g + 1)
        for _ in down(*pending):
            pass
        sp.wait((e_out, e_out.count))

        with nc.Block() as block:
            block.tensor(pe.run)
            block.scalar(act.run)
            block.vector(dve.run)
            block.gpsimd(pool.run)
            block.sync(sp.run)


def rope_tables():
    freqs = (np.float32(1.0) / np.float32(THETA) ** (np.arange(0, HD, 2, dtype=np.float32) / np.float32(HD))).astype(np.float32)
    ang = np.outer(np.arange(S, dtype=np.float32), freqs).astype(np.float32).astype(np.float64)
    cos, sin = np.cos(ang), np.sin(ang)
    c, s = np.concatenate([cos, cos], 1), np.concatenate([-sin, sin], 1)
    k = PROJ_DOWN * QK_UP
    q = k / np.sqrt(HD)
    t = np.stack([c * q, s * q, c * k, s * k], 1).astype(np.float32)
    return np.ascontiguousarray(t.reshape(NT, P, 4, HD).transpose(1, 0, 2, 3))


def masks():
    i = np.arange(P)
    m = np.zeros((P, S), np.float32)
    m[:, S - P:] = np.where(i[None, :] > i[:, None], MASKED, 0.0)
    mt = np.where(i[None, :] < i[:, None], MASKED, 0.0)
    return m, mt


def kernel(**inputs):
    import concourse.bacc as bacc
    from concourse.bass_utils import run_bass_kernel_spmd

    g = {k.replace("L0_", ""): np.asarray(v) for k, v in inputs.items()}
    bf16, f16 = mybir.dt.np(BF16), np.float16
    even_odd = np.concatenate([np.arange(0, HD, 2), np.arange(1, HD, 2)])

    def heads_split(w, n):
        return w.reshape(D, n, HD)[:, :, even_odd].reshape(D, n * HD)

    def chunked(w):
        return w.reshape(KD, P, -1).transpose(1, 0, 2)

    x = g["attn_x"]
    causal, causalT = masks()
    arrays = {
        "xT": x.reshape(B, S, KD, P).transpose(0, 3, 2, 1),
        "x": x.reshape(TILES, P, D),
        "wq": chunked(heads_split(g["attn_wq"], NH)),
        "wkv": chunked(np.concatenate([heads_split(g["attn_wk"], NKV), g["attn_wv"]], 1)),
        "wo": chunked(g["attn_wo"]),
        "gateT": g["ffn_gate_t"].reshape(FC, P, KD, P).transpose(0, 3, 2, 1).reshape(FC, P, D),
        "upT": g["ffn_up_t"].reshape(FC, P, KD, P).transpose(0, 3, 2, 1).reshape(FC, P, D),
        "downT": g["ffn_down_t"].T.reshape(FC, P, D),
        "gate_s": g["ffn_gate_s"].reshape(FC, P).T,
        "up_s": g["ffn_up_s"].reshape(FC, P).T,
        "down_s": g["ffn_down_s"],
        "rope": rope_tables(),
        "causal": causal.astype(bf16),
        "causalT": causalT.astype(bf16),
        "identB": np.eye(P).astype(bf16),
        "identH": np.eye(P).astype(f16),
    }
    arrays = {k: np.ascontiguousarray(v) for k, v in arrays.items()}
    nc = bacc.Bacc("TRN2", target_bir_lowering=False, num_devices=1)
    args = {k: nc.dram_tensor(k, v.shape, mybir.dt.from_np(v.dtype), kind="ExternalInput").ap() for k, v in arrays.items()}
    out = nc.dram_tensor("out", [TILES, P, D], F32, kind="ExternalOutput").ap()
    block_kernel(nc, **args, out=out)
    got = run_bass_kernel_spmd(nc, [arrays], core_ids=[0]).results[0]["out"]
    return np.asarray(got).reshape(B, S, D)
```

```python
from contextlib import ExitStack

import numpy as np
import concourse.bass as bass
from concourse import mybir
from concourse.alu_op_type import AluOpType as ALU

F32, F16, BF16, I32 = mybir.dt.float32, mybir.dt.float16, mybir.dt.bfloat16, mybir.dt.int32
ACT = mybir.ActivationFunctionType

P = 128
B, S, D = 4, 512, 1024
NH, NKV, HD = 32, 8, 32
REP = NH // NKV
FF = 3584
KD = D // P
NT = S // P
TILES = B * NT
HALF = 512
UH = 8
UNITS = NH // UH
UG = UH // REP
FC = FF // P
GC = 4
EPS = 1e-5
THETA = 10000.0

STK = 3 * HD
STKM = STK + 2

X_UP, W_UP = 2.0 ** 6, 2.0 ** 8
PROJ_DOWN = 1.0 / (X_UP * W_UP)
QK_UP = 2.0 ** 4
ATT_UP = 2.0 ** 6
OUT_DOWN = 1.0 / (ATT_UP * W_UP)
SCORE_DOWN = 1.0 / QK_UP ** 2
MAX_ONE = QK_UP ** 2
X1_UP = 2.0 ** 10
HID_BOUND = float(D) ** 2 / 2.0 ** 15
MASKED = -1.0e30


class Event:

    def __init__(self, sem):
        self.sem, self.count = sem, 0


class Queue:

    def __init__(self):
        self.todo, self.seen = [], {}

    def wait(self, *tickets):
        for t in tickets:
            if t is None:
                continue
            event, count = t
            if self.seen.get(id(event), 0) < count:
                self.seen[id(event)] = count
                self.todo.append(lambda e, s=event.sem, c=count: e.wait_ge(s, c))

    def do(self, make, event=None, by=1):
        if event is None:
            self.todo.append(lambda e, m=make: m(e))
            return None
        event.count += by
        self.todo.append(lambda e, m=make, s=event.sem, n=by: m(e).then_inc(s, n))
        return event, event.count

    def run(self, e):
        for step in self.todo:
            step(e)


class Order:

    def __init__(self):
        self.now, self.later, self.n = 0.0, [], 0

    def after(self, delay, stage):
        self.n += 1
        self.later.append((self.now + delay, self.n, stage))

    def follow_up(self):
        due = min(self.later, key=lambda f: f[:2])
        self.later.remove(due)
        self.now = max(self.now, due[0])
        said = due[2]()
        if said is BLOCKED:
            self.after(300, due[2])
        else:
            self.now += said or 0

    def run(self, streams, until=None):
        waiting = [[s, 0.0] for s in streams]
        blocked = 0
        while waiting or self.later:
            if until is not None and until():
                return
            next_due = min((f[0] for f in self.later), default=None)
            if next_due is not None and next_due <= self.now:
                self.follow_up()
                continue
            for w in sorted(waiting, key=lambda w: w[1] > self.now and w[1]):
                if next_due is not None and w[1] > max(next_due, self.now):
                    continue
                started = max(self.now, w[1])
                said = next(w[0], None)
                if said is BLOCKED:
                    continue
                if said is None:
                    waiting.remove(w)
                else:
                    self.now = started + said[0]
                    w[1] = started + said[1]
                blocked = 0
                break
            else:
                blocked += 1
                if next_due is None or blocked > 1000:
                    raise RuntimeError("every stream is blocked")
                self.follow_up()


BLOCKED = "blocked"


def block_kernel(nc, xT, x, wq, wkv, wo, gateT, upT, downT, gate_s, up_s, down_s,
                 rope, causal, identH, out):
    x1_dram = nc.dram_tensor("x1_spill", [TILES, P, D], F32, kind="Internal").ap()
    x1T_dram = nc.dram_tensor("x1T_spill", [TILES, P, 2 * KD * P], F16, kind="Internal").ap()

    ctx = ExitStack()
    with ctx:
        pe, act, dve, pool, sp = (Queue() for _ in range(5))

        def ev(name):
            return Event(ctx.enter_context(nc.semaphore(name)))

        def psum(name, dt=F32, cols=HALF):
            return ctx.enter_context(nc.psum_tensor(name, [P, cols], dt))

        def sb(where, name, shape, dt):
            return where.enter_context(nc.sbuf_tensor(name, [P, *shape], dt))

        bank = [psum(f"bank{i}") for i in range(8)]

        KEPT = 5
        page = [sb(ctx, f"page{i}", [D], F32) for i in range(KEPT)]
        idH = sb(ctx, "idH", [P], F16)
        stats = sb(ctx, "stats", [2, 2, 6], F32)
        mv = sb(ctx, "mv", [2, 2], F32)
        rstd = sb(ctx, "rstd", [2, 3], F32)

        NPAGE = 6
        A = ctx.enter_context(ExitStack())
        page += [sb(A, f"page{i}", [D], F32) for i in range(KEPT, NPAGE)]
        page_ev = [ev(f"page{i}_dma") for i in range(NPAGE)]
        free_pages = [(i, ()) for i in range(NPAGE)]

        def take_page():
            return free_pages.pop(0)

        def give_page(i, *tickets):
            free_pages.append((i, tickets))

        def load(dst, src, event, queue=None, waits=()):
            q = queue or sp
            q.wait(*waits)
            return q.do(lambda e: e.dma_start(dst, src), event, 16)

        def load_page(src, view):
            i, before = take_page()
            return i, load(view(page[i]), src, page_ev[i], waits=before)

        order = Order()

        e_ln, e_lnpool = ev("ln_step"), ev("ln_newton")
        pool_last = [None]
        ln_last = [(), ()]

        def layernorm(row, slot, ready, then):
            if ln_last[slot] is None:
                return BLOCKED
            before, ln_last[slot] = ln_last[slot], None
            dve.wait(ready, *before)
            for h in range(2):
                t = dve.do(lambda e, h=h: nc.vector.bn_stats(stats[:, slot, h, :], row[:, h * HALF:(h + 1) * HALF]), e_ln)
            dve.wait(t)
            t = dve.do(lambda e: nc.vector.bn_aggr(mv[:, slot, :], stats[:, slot, :, :]), e_ln)
            v, r, w = rstd[:, slot, 0:1], rstd[:, slot, 1:2], rstd[:, slot, 2:3]
            dve.wait(t)
            t = dve.do(lambda e: nc.vector.tensor_scalar(v, mv[:, slot, 1:2], EPS, None, ALU.add), e_ln)
            dve.wait(t)
            t = dve.do(lambda e: nc.vector.tensor_scalar(r.bitcast(I32), v.bitcast(I32), -0.5, float(0x5F3759DF),
                                                         ALU.mult, ALU.add), e_ln)
            pool.wait(t, pool_last[0])
            for _ in range(3):
                for step in (lambda e: nc.gpsimd.tensor_tensor(w, r, r, ALU.mult),
                             lambda e: nc.gpsimd.tensor_tensor(w, w, v, ALU.mult),
                             lambda e: nc.gpsimd.tensor_scalar(w, w, -0.5, 1.5, ALU.mult, ALU.add),
                             lambda e: nc.gpsimd.tensor_tensor(r, r, w, ALU.mult)):
                    t = pool_last[0] = pool.do(step, e_lnpool)
                    pool.wait(t)

            def rest():
                dve.wait(t)
                n = dve.do(lambda e: nc.vector.tensor_scalar(row, row, mv[:, slot, 0:1], r,
                                                             ALU.subtract, ALU.mult), e_ln)
                ln_last[slot] = (n,)
                order.after(0, lambda: then(n))

            order.after(5500, rest)

        wq_p = sb(A, "wq_parts", [2, KD, D], F16)
        wkv_p = sb(A, "wkv_parts", [2, KD, 2 * NKV * HD], F16)
        xT_p = sb(A, "xT_parts", [2, KD, S], F16)
        qT = sb(A, "q_stack", [2, UH, S], F16)
        kT = sb(A, "k_stack", [2, NKV, S], F16)
        v32 = sb(A, "v32", [2, NT, NKV * HD], F32)
        NNAT = 3
        nat = sb(A, "stack_rows", [NNAT, UH, STK], F16)
        ropeA = sb(A, "rope_cos", [NNAT, UH * HD], F32)
        ropeB = sb(A, "rope_sin", [NNAT, UH * HD], F32)
        NP32 = 7
        p32 = sb(A, "p32", [NP32, S], F32)
        tab = sb(A, "rope_tab", [NT, 4, HD], F32)
        cmask = sb(A, "cmask", [S], BF16)
        ones = sb(A, "ones", [HD], F32)
        mx = sb(A, "row_max", [2, NT, UH], F32)
        mneg = sb(A, "neg_max", [NT, UH], F32)
        m_p = sb(A, "max_parts", [NT, 2, UH], F16)
        mT = sb(A, "max_rows", [S], F16)

        wo_p = sb(A, "wo_parts", [2, KD, D], F16)
        att = sb(A, "att_parts", [2, KD, S], F16)

        e_const, e_const2 = ev("const_dma"), ev("const_set")
        consts = None
        for dst, src in ((idH[:, :], identH), (cmask[:, :], causal),
                         (tab[:, :, :, :], rope)):
            consts = load(dst, src, e_const, act)
        pool.wait(pool.do(lambda e: nc.gpsimd.memset(ones[:, :], 1.0), e_const2))
        const_set = pool_last[0] = pool.do(lambda e: nc.gpsimd.memset(kT[96:128, :, :, :], MAX_ONE), e_const2)

        e_hi, e_lo = ev("split_hi"), ev("split_lo")

        def split_page(i, arrived, hi, lo, up, ready, keys, before=()):
            src = page[i][:, :]

            def split_hi():
                act.wait(arrived, *before)
                h = act.do(lambda e: nc.scalar.activation(hi, src, ACT.Copy, scale=up), e_hi)

                def split_lo():
                    dve.wait(arrived, h, *before)
                    l = dve.do(lambda e: nc.vector.scalar_tensor_tensor(lo, src, up, hi, ALU.mult, ALU.subtract), e_lo)
                    give_page(i, h, l)
                    ready.update((key, l) for key in keys)

                order.after(1000, split_lo)

            order.after(3000, split_hi)

        def flat(ap):
            return ap.rearrange("p a b -> p (a b)")

        xT_ready = {}
        xT_free = [()]

        def load_pair(w, k, parts, up, ready, keys, before=()):
            while not free_pages:
                yield BLOCKED
            i, t = load_page(w[:, k:k + 2, :], lambda pg: pg[:, :].rearrange("p (a b) -> p a b", a=2))
            split_page(i, t, flat(parts[:, 0, k:k + 2, :]), flat(parts[:, 1, k:k + 2, :]), up, ready, keys, before)
            yield 0, 0

        def load_x(b, k):
            return load_pair(xT[b], k, xT_p, X_UP, xT_ready, [(b, k), (b, k + 1)], xT_free[0])

        wkv_ready, wq_ready, wo_ready = {}, {}, {}

        def load_square(w, parts, ready, gap):
            for k in range(KD):
                while not free_pages:
                    yield BLOCKED
                i, t = load_page(w[:, k, :], lambda pg: pg[:, :])
                split_page(i, t, parts[:, 0, k, :], parts[:, 1, k, :], W_UP, ready, [k])
                yield 0, gap

        def first_loads():
            for k in range(0, KD, 2):
                yield from load_x(0, k)
                yield from load_pair(wkv, k, wkv_p, W_UP, wkv_ready, [k, k + 1])
            yield from load_square(wq, wq_p, wq_ready, 0)
            yield from load_square(wo, wo_p, wo_ready, 1200)

        readers = {i: () for i in range(8)}
        PROJ, TRANS, SCORE, PV, DEN = (0, 1), (2,), (3, 4, 5), 6, 7
        turn = {PROJ: 0, SCORE: 0}

        def pending(ring):
            return readers[ring[turn[ring] % len(ring)]] is None

        def next_bank(ring):
            i = ring[turn[ring] % len(ring)]
            turn[ring] += 1
            return i

        e_proj, e_rope, e_ropep, e_nathi, e_natlo = ev("proj"), ev("rope"), ev("rope_sum"), ev("nat_hi"), ev("nat_lo")
        e_tr, e_trc = ev("transposed"), ev("stack_copied")
        nat_turn = [0]
        nat_readers = [()] * NNAT
        rope_readers = [()] * NNAT

        def three_passes(dst, lhs, rhs, ready, cols):
            for k in range(KD):
                while None in ready(k):
                    yield BLOCKED
                pe.wait(*ready(k))
                for n, (a, c) in enumerate(((0, 0), (0, 1), (1, 0))):
                    first, last = k == 0 and n == 0, k == KD - 1 and n == 2
                    t = pe.do(lambda e, left=lhs(a, k), right=rhs(c, k), first=first, last=last:
                              nc.tensor.matmul(dst, left, right, start=first, stop=last), e_proj if last else None)
                yield 3 * cols / 2.4, 0
            return t

        def rotate(bk, nh, t, kind, ready, then):
            s = nat_turn[0] % NNAT
            if nat_readers[s] is None:
                return BLOCKED
            nat_turn[0] += 1
            before_nat, nat_readers[s] = nat_readers[s], None
            src = bank[bk][:, 0:nh * HD].rearrange("p (h c) -> p h c", h=nh)
            ta = ropeA[:, s, 0:nh * HD].rearrange("p (h c) -> p h c", h=nh)
            tb = ropeB[:, s, 0:nh * HD].rearrange("p (h c) -> p h c", h=nh)
            q = HD // 2

            def tabled(n, lo, hi):
                return tab[:, t:t + 1, 2 * kind + n, lo:hi].broadcast_to([P, nh, hi - lo])

            dve.wait(ready, consts, *rope_readers[s])
            dve.do(lambda e: nc.vector.tensor_tensor(ta, src, tabled(0, 0, HD), ALU.mult))
            dve.do(lambda e: nc.vector.tensor_tensor(tb[:, :, 0:q], src[:, :, q:HD], tabled(1, 0, q), ALU.mult))
            r = dve.do(lambda e: nc.vector.tensor_tensor(tb[:, :, q:HD], src[:, :, 0:q], tabled(1, q, HD), ALU.mult), e_rope)
            readers[bk] = (r,)
            pool.wait(r, pool_last[0])
            r = pool_last[0] = pool.do(lambda e: nc.gpsimd.tensor_tensor(
                ropeA[:, s, 0:nh * HD], ropeA[:, s, 0:nh * HD], ropeB[:, s, 0:nh * HD], ALU.add), e_ropep)
            rows = nat[:, s, 0:nh, :].rearrange("p h (f c) -> p h f c", f=3)
            field = (slice(0, 3, 2), 1) if kind else (slice(0, 2), 2)

            def split_hi():
                act.wait(r, *before_nat)
                h = act.do(lambda e: nc.scalar.activation(
                    rows[:, :, field[0], :], ta.unsqueeze(2).broadcast_to([P, nh, 2, HD]), ACT.Copy), e_nathi)

                def split_lo():
                    dve.wait(r, h)
                    l = dve.do(lambda e: nc.vector.tensor_tensor(rows[:, :, field[1], :], ta, rows[:, :, 0, :],
                                                                 ALU.subtract), e_natlo)
                    rope_readers[s] = (h, l)
                    order.after(700, lambda: then(s, l))

                order.after(800, split_lo)

            order.after(2100, split_hi)

        def transpose_heads(s, nh, ready, dst, before):
            tb = bank[TRANS[0]][:, :].bitcast(F16).rearrange("p (h c) -> p h c", h=8)
            pe.wait(ready, consts, *readers[TRANS[0]])
            for h in range(nh):
                t = pe.do(lambda e, h=h: nc.tensor.transpose(tb[0:STK, h, :], nat[:, s, h, :], idH[:, :]),
                          e_tr if h == nh - 1 else None)
            nat_readers[s] = (t,)
            dve.wait(t, *before)
            c = dve.do(lambda e: nc.vector.tensor_copy(dst, tb[0:STK, 0:nh, :]), e_trc)
            readers[TRANS[0]] = (c,)
            return c

        k_ready, v_ready, q_ready = {}, {}, {}
        st_done = {}
        pv_done = {}
        e_v = ev("v")

        def project(u, with_kv):
            b, g = divmod(u, UNITS)
            while u - 2 not in attended and u >= 2:
                yield BLOCKED
            for what, t in ([("kv", t) for t in range(NT)] if with_kv else []) + [("q", t) for t in range(NT)]:
                while pending(PROJ):
                    yield BLOCKED
                bk = next_bank(PROJ)
                pe.wait(*readers[bk])
                readers[bk] = None
                rows = slice(t * P, (t + 1) * P)
                if what == "kv":
                    done = yield from three_passes(bank[bk][:, :], lambda a, k: xT_p[:, a, k, rows],
                                        lambda c, k: wkv_p[:, c, k, :], lambda k: (xT_ready.get((b, k)), wkv_ready.get(k)), HALF)
                    nh, record, key = NKV, k_ready, (b, t)
                    dst, before = kT[0:STK, b % 2, :, rows], (b - 1) * UNITS - 1
                else:
                    done = yield from three_passes(bank[bk][:, 0:UH * HD], lambda a, k: xT_p[:, a, k, rows],
                                        lambda c, k: wq_p[:, c, k, g * UH * HD:(g + 1) * UH * HD],
                                        lambda k: (xT_ready.get((b, k)), wq_ready.get(k)), UH * HD)
                    nh, record, key = UH, q_ready, (u, t)
                    dst, before = qT[0:STK, u % 2, :, rows], u - 2
                    if t == NT - 1 and g == UNITS - 1:
                        xT_free[0] = (done,)

                def transpose(s, ready, nh=nh, dst=dst, before=before, record=record, key=key):
                    record[key] = transpose_heads(s, nh, ready, dst, [st_done.get(before)])
                    return nh * 60

                def receive(what=what, t=t, bk=bk, done=done, nh=nh, transpose=transpose):
                    if what == "q":
                        return rotate(bk, nh, t, 0, done, transpose)
                    nk = NKV * HD
                    act.wait(done, pv_done.get((b - 1) * UNITS - 1))
                    vt = v32[:, b % 2, t, :]
                    h = v_ready[b, t] = act.do(lambda e: nc.scalar.activation(
                        vt, bank[bk][:, nk:2 * nk], ACT.Copy, scale=PROJ_DOWN), e_v)
                    order.after(500, lambda: rotate(bk, nh, t, 1, h, transpose))

                order.after(300, receive)

        e_smax, e_mx, e_mpart, e_mtr, e_mcopy = ev("score_q"), ev("row_max"), ev("max_part"), ev("max_tr"), ev("max_copy")
        e_mrow = [ev("max_rows_dma0"), ev("max_rows_dma1")]
        m_ready, m_there = {}, set()

        def maxima(u):
            b, g = divmod(u, UNITS)
            for i in range(NT):
                n = (i + 1) * P
                while (u, i) not in q_ready or (b, i) not in k_ready:
                    yield BLOCKED
                yield 0, 1400
                for h in range(UH):
                    kv = (g * UH + h) // REP
                    bk = next_bank(SCORE)
                    pe.wait(q_ready[u, i], k_ready[b, i], *readers[bk])
                    t = pe.do(lambda e, bk=bk, h=h, kv=kv, i=i, n=n: nc.tensor.matmul(
                        bank[bk][:, 0:n], qT[0:STK, u % 2, h, i * P:n], kT[0:STK, b % 2, kv, 0:n],
                        start=True, stop=True), e_smax)
                    dve.wait(t)
                    r = dve.do(lambda e, bk=bk, h=h, i=i, n=n: nc.vector.tensor_tensor_reduce(
                        out=bank[bk][:, 0:n], in0=bank[bk][:, 0:n], in1=cmask[:, S - n:S], scale=1.0, scalar=MASKED,
                        op0=ALU.add, op1=ALU.max, accum_out=mx[:, u % 2, i, h:h + 1]), e_mx)
                    readers[bk] = (r,)
                    yield n / 2.4 + 3, n / 0.96 + 80
            dve.wait(r, m_ready.get(("tr", u - 1)))
            mm = mx[:, u % 2, :, :]
            a = dve.do(lambda e: nc.vector.tensor_scalar(mneg[:, :, :], mm, -1.0 / MAX_ONE, None, ALU.mult), e_mpart)
            dve.wait(a)
            a = dve.do(lambda e: nc.vector.tensor_copy(m_p[:, :, 0, :], mneg[:, :, :]), e_mpart)
            dve.wait(a)
            a = dve.do(lambda e: nc.vector.tensor_tensor(m_p[:, :, 1, :], mneg[:, :, :], m_p[:, :, 0, :], ALU.subtract), e_mpart)

            def transpose():
                tb = bank[TRANS[0]][:, :].bitcast(F16)
                pe.wait(a, *readers[TRANS[0]])
                for i in range(NT):
                    t = pe.do(lambda e, i=i: nc.tensor.transpose(tb[0:2 * UH, i * P:(i + 1) * P],
                                                                 m_p[:, i, :, :].rearrange("p a h -> p (a h)"), idH[:, :]),
                              e_mtr if i == NT - 1 else None)
                m_ready["tr", u] = t
                dve.wait(t, *m_ready.get(("dma", u - 1), ()))
                c = dve.do(lambda e: nc.vector.tensor_copy(mT[0:2 * UH, :], tb[0:2 * UH, 0:S]), e_mcopy)
                readers[TRANS[0]] = (c,)
                both = []
                for n in range(2):
                    both.append(load(qT[STK + n:STK + n + 1, u % 2, :, :], mT[n * UH:(n + 1) * UH, :], e_mrow[n], sp,
                                     waits=(c, st_done.get(u - 2))))
                m_ready["dma", u] = m_ready[u] = tuple(both)
                order.after(4500, lambda: m_there.add(u))
                return 250

            order.after(1000, transpose)
            yield 0, 0

        e_st, e_exp, e_causal, e_pv, e_den = ev("score_k"), ev("exp"), ev("causal"), ev("pv"), ev("den")
        e_take, e_rden, e_att, e_atthi, e_attlo = ev("pv_taken"), ev("rden"), ev("att"), ev("att_hi"), ev("att_lo")
        p32_readers = [()] * NP32
        p_turn = [0]
        att_ready, att_free = {}, {-1: ()}

        def attend(u):
            b, g = divmod(u, UNITS)

            def pv(G, j, slots, ready):
                lo = j * P
                kv = g * UG + G
                pe.wait(v_ready[b, j], const_set, *ready)
                if j == 0:
                    pe.wait(*readers[PV], *readers[DEN])
                for dst, lhs, event in ((PV, v32[:, b % 2, j, kv * HD:(kv + 1) * HD], e_pv), (DEN, ones[:, :], e_den)):
                    for hh in range(REP):
                        t = pe.do(lambda e, dst=dst, hh=hh, lhs=lhs, sl=slots[hh]: nc.tensor.matmul(
                            bank[dst][hh * HD:(hh + 1) * HD, lo:S], lhs, p32[:, sl, lo:S], start=j == 0,
                            stop=j == NT - 1, tile_position=(0, hh * HD)), event if hh == REP - 1 else None)
                for s in slots:
                    p32_readers[s] = (t,)
                pv_done[u] = t
                cost = 8 * ((S - lo) * 0.45 + 5)
                if j == NT - 1:
                    readers[PV] = readers[DEN] = None
                    order.after(cost + 0, lambda: normalise(G, t))
                return cost

            def normalise(G, done):
                gg = g * UG + G
                if b - 1 not in att_free or not free_pages:
                    return BLOCKED
                i, before = take_page()
                den, pvs = page[i][:, 0:S], page[i][:, S:2 * S]
                act.wait(done, *before)
                d = act.do(lambda e: nc.scalar.activation(den, bank[DEN][:, :], ACT.Copy), e_take)
                a = act.do(lambda e: nc.scalar.activation(pvs, bank[PV][:, :], ACT.Copy, scale=ATT_UP), e_take)
                readers[PV] = readers[DEN] = (a,)

                def invert(c):
                    q = den[:, c * P:(c + 1) * P]
                    dve.wait(d)
                    r = dve.do(lambda e: nc.vector.reciprocal(q, q), e_rden)
                    order.after(2200, (lambda: invert(c + 1)) if c < NT - 1 else (lambda: multiply(r)))

                def multiply(r):
                    dve.wait(r, a)
                    m = dve.do(lambda e: nc.vector.tensor_tensor(pvs, pvs, den, ALU.mult), e_att)
                    act.wait(m, *att_free[b - 1])
                    h = act.do(lambda e: nc.scalar.activation(att[:, 0, gg, :], pvs, ACT.Copy), e_atthi)

                    def split_lo():
                        dve.wait(h)
                        l = dve.do(lambda e: nc.vector.tensor_tensor(att[:, 1, gg, :], pvs, att[:, 0, gg, :],
                                                                     ALU.subtract), e_attlo)
                        give_page(i, l)
                        att_ready[b, gg] = l

                    order.after(1400, split_lo)

                order.after(800, lambda: invert(0))

            late = None
            for G in range(UG):
                kv = g * UG + G
                for j in range(NT):
                    lo = j * P
                    slots, ready = [], []
                    for hh in range(REP):
                        h = G * REP + hh
                        while u not in m_there:
                            yield BLOCKED
                        bk = next_bank(SCORE)
                        pe.wait(*m_ready[u], const_set, *[q_ready[u, i] for i in range(j, NT)], k_ready[b, j], *readers[bk])
                        t = pe.do(lambda e, bk=bk, h=h, lo=lo, kv=kv: nc.tensor.matmul(
                            bank[bk][:, 0:S - lo], kT[0:STKM, b % 2, kv, lo:lo + P], qT[0:STKM, u % 2, h, lo:S],
                            start=True, stop=True), e_st)
                        st_done[u] = t
                        a = p_turn[0] % NP32
                        p_turn[0] += 1
                        act.wait(t, *p32_readers[a])
                        x_ = act.do(lambda e, bk=bk, a=a, lo=lo: nc.scalar.activation(
                            p32[:, a, lo:S], bank[bk][:, 0:S - lo], ACT.Exp, scale=SCORE_DOWN), e_exp)
                        readers[bk] = (x_,)
                        pool.wait(x_, pool_last[0])
                        m_ = pool_last[0] = pool.do(lambda e, a=a, lo=lo: nc.gpsimd.affine_select(
                            out=p32[:, a, lo:lo + P], in_=p32[:, a, lo:lo + P], compare_op=ALU.is_ge, fill=0.0,
                            base=0, pattern=[[1, P]], channel_multiplier=-1), e_causal)
                        slots.append(a)
                        ready.append(m_)
                        yield (S - lo) / 2.4 + 3, (S - lo) / 1.2 + 310
                        if hh == 1 and late:
                            while late[1] == 0 and readers[PV] is None:
                                yield BLOCKED
                            yield pv(*late), 0
                            late = None
                    late = (G, j, slots, ready)
            attended.add(u)
            yield 0, 1000
            yield pv(*late), 0

        attended = set()

        e_res, e_x1hi, e_x1lo, e_x1tr, e_x1c = ev("residual"), ev("x1_hi"), ev("x1_lo"), ev("x1_tr"), ev("x1_copy")
        x1_stored, x1T_stored = {}, {}
        sent = []

        def output(b):
            while any((b, gg) not in att_ready for gg in range(KD)):
                yield BLOCKED

            def store_transposed(tile, i, l):
                if not free_pages:
                    return BLOCKED
                o, before = take_page()
                parts = page[i][:, :].bitcast(F16).rearrange("p (a k c) -> p a k c", a=2, k=KD)
                dst = page[o][:, :].bitcast(F16).rearrange("p (a k c) -> p a k c", a=2, k=KD)
                tb = bank[TRANS[0]][:, :].bitcast(F16).rearrange("p (h c) -> p h c", h=KD)

                def part(a):
                    pe.wait(l, *readers[TRANS[0]])
                    for k in range(KD):
                        t = pe.do(lambda e, k=k: nc.tensor.transpose(tb[:, k, :], parts[:, a, k, :], idH[:, :]),
                                  e_x1tr if k == KD - 1 else None)
                    act.wait(t, *before)
                    c = act.do(lambda e: nc.scalar.activation(dst[:, a, :, :], tb[:, :, :], ACT.Copy), e_x1c)
                    readers[TRANS[0]] = (c,)
                    if a == 0:
                        order.after(2000, lambda: part(1))
                    else:
                        give_page(i, t)
                        s = load(x1T_dram[tile], page[o][:, :].bitcast(F16), page_ev[o], sp, waits=(c,))
                        x1T_stored[tile] = s
                        give_page(o, s)
                    return 8 * 60

                return part(0)

            def split_x1(tile, i, row, n):
                s = load(x1_dram[tile], row, page_ev[i], sp, waits=(n,))
                x1_stored[tile] = s
                o, before = take_page()
                hi, lo = page[o][:, 0:HALF].bitcast(F16), page[o][:, HALF:D].bitcast(F16)
                act.wait(n, *before)
                h = act.do(lambda e: nc.scalar.activation(hi, row, ACT.Copy, scale=X1_UP), e_x1hi)

                def split_lo():
                    dve.wait(h, *before)
                    l = dve.do(lambda e: nc.vector.scalar_tensor_tensor(lo, row, X1_UP, hi, ALU.mult, ALU.subtract), e_x1lo)
                    give_page(i, s, h, l)
                    order.after(1800, lambda: store_transposed(tile, o, l))

                order.after(1200, split_lo)

            for t in range(NT):
                tile = b * NT + t
                while len(free_pages) < 3:
                    yield BLOCKED
                i, arrived = load_page(x[tile], lambda pg: pg[:, :])
                row = page[i][:, :]
                for h in range(2):
                    cols = slice(h * HALF, (h + 1) * HALF)
                    while pending(PROJ):
                        yield BLOCKED
                    bk = next_bank(PROJ)
                    pe.wait(*readers[bk])
                    readers[bk] = None
                    done = yield from three_passes(bank[bk][:, :], lambda a, k: att[:, a, k, t * P:(t + 1) * P],
                                        lambda c, k: wo_p[:, c, k, cols], lambda k: (att_ready[b, k], wo_ready.get(k)), HALF)

                    def receive(h=h, bk=bk, done=done, row=row, cols=cols, arrived=arrived, tile=tile, i=i):
                        dve.wait(done, arrived)
                        r = dve.do(lambda e: nc.vector.scalar_tensor_tensor(
                            row[:, cols], bank[bk][:, :], OUT_DOWN, row[:, cols], ALU.mult, ALU.add), e_res)
                        readers[bk] = (r,)
                        if h:
                            order.after(0, lambda: layernorm(
                                row, tile % 2, r, lambda n: split_x1(tile, i, row, n) if free_pages else BLOCKED))

                    order.after(100, receive)
            att_free[b] = (done,)

        NU = B * UNITS

        def all_units(stage):
            for u in range(NU):
                yield from stage(u)

        def projections():
            for u in range(NU):
                if u and u % UNITS == 0:
                    for k in range(0, KD, 2):
                        yield from load_x(u // UNITS, k)
                yield from project(u, u % UNITS == 0)

        def outputs():
            for b in range(B - 1):
                yield from output(b)

        order.run([all_units(attend), first_loads(), all_units(maxima), outputs(),
                   projections()], until=lambda: len(att_ready) == B * KD)

        extra = [(i, ts) for i, ts in free_pages if i >= KEPT]
        assert len(extra) == NPAGE - KEPT
        free_pages[:] = [(i, ts) for i, ts in free_pages if i < KEPT]
        A.close()
        over = tuple(t for _, ts in extra for t in ts) + tuple(
            (e, e.count) for e in (e_proj, e_rope, e_ropep, e_nathi, e_natlo, e_tr, e_trc, e_v, e_hi, e_lo, e_smax, e_mx,
                                   e_mpart, e_mtr, e_mcopy, e_st, e_exp, e_causal, e_pv, e_den, e_atthi, e_attlo, *e_mrow))

        BB = ctx.enter_context(ExitStack())
        x1T = sb(BB, "x1T", [TILES, 2, KD, P], F16)
        NW = 6
        w_gate = sb(BB, "w_gate", [NW, KD, P], F16)
        w_up = sb(BB, "w_up", [NW, KD, P], F16)
        w_down = sb(BB, "w_down", [NW, D], F16)
        hid = sb(BB, "hid", [2, GC, 2, S], F16)
        silu = sb(BB, "silu", [2, S], F32)
        sg = sb(BB, "sg", [FC], F32)
        su = sb(BB, "su", [FC], F32)
        sc = sb(BB, "sc", [8], F32)
        bias = sb(BB, "bias", [2, 1], F32)
        acc = sb(BB, "acc", [TILES, D], F32)

        e_sc, e_sdma = ev("scales"), ev("scale_dma")
        load(sg[:, :], gate_s, e_sdma, sp, waits=over)
        s_in = load(su[:, :], up_s, e_sdma, sp)
        RMAX = bass.bass_isa.ReduceOp.max
        dve.wait(s_in, *over)
        dve.do(lambda e: nc.vector.tensor_reduce(sc[:, 0:1], sg[:, :], mybir.AxisListType.X, ALU.max,
                                                 apply_absolute_value=True))
        t = dve.do(lambda e: nc.vector.tensor_reduce(sc[:, 1:2], su[:, :], mybir.AxisListType.X, ALU.max,
                                                     apply_absolute_value=True), e_sc)
        pool.wait(t, pool_last[0])
        t = pool.do(lambda e: nc.gpsimd.partition_all_reduce(sc[:, 2:4], sc[:, 0:2], P, RMAX), e_sc)
        dve.wait(t)
        t = dve.do(lambda e: nc.vector.tensor_scalar(sc[:, 4:5], sc[:, 2:3], sc[:, 3:4], HID_BOUND, ALU.mult, ALU.mult), e_sc)
        dve.wait(t)
        t = dve.do(lambda e: nc.vector.tensor_scalar(sc[:, 5:6], sc[:, 4:5], 1e-30, None, ALU.max), e_sc)
        dve.wait(t)
        t = dve.do(lambda e: nc.vector.reciprocal(sc[:, 6:7], sc[:, 5:6]), e_sc)
        dve.wait(t)
        dve.do(lambda e: nc.vector.tensor_scalar(sg[:, :], sg[:, :], 1.0 / X1_UP, None, ALU.mult))
        scales = dve.do(lambda e: nc.vector.tensor_scalar(su[:, :], su[:, :], sc[:, 6:7], 1.0 / X1_UP, ALU.mult, ALU.mult), e_sc)

        e_w = ev("weights_cast")
        w_ready = {}

        def weights(c, kinds, free):
            for kind in kinds:
                w, dst = ((gateT, w_gate), (upT, w_up), (downT, w_down))[kind]
                while not free_pages:
                    yield BLOCKED
                i, before = take_page()
                pg = page[i][:, :].bitcast(I32)
                arrived = load(pg, w[c], page_ev[i], sp, waits=before)
                to = dst[:, c % NW, :] if kind == 2 else flat(dst[:, c % NW, :, :])

                def cast(i=i, kind=kind, to=to, pg=pg, arrived=arrived):
                    act.wait(arrived, *free)
                    t = act.do(lambda e: nc.scalar.activation(to, pg, ACT.Copy), e_w)
                    give_page(i, t)
                    w_ready[c, kind] = t

                order.after(3500, cast)
                yield 0, 0

        e_x1T = [ev(f"x1T_load{t}") for t in range(B)]
        x1T_ready = {}

        def load_x1T():
            for t in range(TILES):
                while t not in x1T_stored:
                    yield BLOCKED
                x1T_ready[t // NT] = load(x1T[:, t, :, :, :].rearrange("p a k c -> p (a k c)"), x1T_dram[t],
                                          e_x1T[t // NT], sp, waits=(x1T_stored[t], *over))
                yield 0, 5000

        GATE, UP, DOWN = (4, 5), (6, 7), (0, 1, 2, 3)
        for r in (GATE, UP, DOWN):
            turn[r] = 0
        e_gu, e_silu, e_h, e_hhi, e_hlo = ev("gate_up"), ev("silu"), ev("hidden"), ev("hid_hi"), ev("hid_lo")
        e_down, e_acc, e_fin = ev("down"), ev("acc"), ev("final")
        silu_readers, hid_readers = [over] * 2, [over] * 2
        small = [0]
        acc_ready = {}

        def gate_up(g, tb, slot, hid_ready):
            for c in range(GC):
                ch = g * GC + c
                w = ch % NW
                gb, ub = next_bank(GATE), next_bank(UP)
                for kind, bk, ws in ((0, gb, w_gate), (1, ub, w_up)):
                    while (ch, kind) not in w_ready:
                        yield BLOCKED
                    pe.wait(w_ready[ch, kind], x1T_ready[tb], *readers[bk])
                    for k in range(KD):
                        for a in range(2):
                            t = pe.do(lambda e, bk=bk, ws=ws, w=w, k=k, a=a: nc.tensor.matmul(
                                bank[bk][:, :], ws[:, w, k, :], x1T[:, tb * NT:(tb + 1) * NT, a, k, :],
                                start=(k == 0 and a == 0), stop=(k == KD - 1 and a == 1)),
                                e_gu if k == KD - 1 and a == 1 else None)
                    if kind == 0:
                        gt = t
                s = small[0] % 2
                small[0] += 1
                act.wait(gt, scales, *silu_readers[s])
                x_ = act.do(lambda e, gb=gb, ch=ch, s=s: nc.scalar.activation(silu[:, s, :], bank[gb][:, :], ACT.Silu,
                                                                              scale=sg[:, ch:ch + 1]), e_silu)
                readers[gb] = (x_,)
                dve.wait(t, x_)
                h = dve.do(lambda e, ub=ub, ch=ch, s=s: nc.vector.scalar_tensor_tensor(
                    silu[:, s, :], bank[ub][:, :], su[:, ch:ch + 1], silu[:, s, :], ALU.mult, ALU.mult), e_h)
                readers[ub] = (h,)
                act.wait(h, *hid_readers[slot])
                hi = act.do(lambda e, c=c, s=s: nc.scalar.activation(hid[:, slot, c, 0, :], silu[:, s, :], ACT.Copy), e_hhi)
                dve.wait(hi)
                l = dve.do(lambda e, c=c, s=s: nc.vector.tensor_tensor(hid[:, slot, c, 1, :], silu[:, s, :],
                                                                       hid[:, slot, c, 0, :], ALU.subtract), e_hlo)
                silu_readers[s] = (hi, l)
                hid_ready.append(l)
                yield 32 * 216, 0
            if tb == B - 1:
                gu_last[g] = t

        def down(g, tb, slot, hid_ready):
            if g == NG - 1 and tb == 0:
                while to_add:
                    add_x1()
                last_page.extend(take_page() for _ in range(2))
            for i in range(NT):
                tile = tb * NT + i
                for h in range(2):
                    cols = slice(h * HALF, (h + 1) * HALF)
                    bk = next_bank(DOWN)
                    pe.wait(*readers[bk], *hid_ready)
                    for c in range(GC):
                        ch = g * GC + c
                        while (ch, 2) not in w_ready:
                            yield BLOCKED
                        pe.wait(w_ready[ch, 2])
                        for a in range(2):
                            t = pe.do(lambda e, bk=bk, c=c, a=a, i=i, ch=ch, cols=cols: nc.tensor.matmul(
                                bank[bk][:, :], hid[:, slot, c, a, i * P:(i + 1) * P], w_down[:, ch % NW, cols],
                                start=(c == 0 and a == 0), stop=(c == GC - 1 and a == 1)),
                                e_down if c == GC - 1 and a == 1 else None)
                    dst = acc[:, tile, cols]
                    if g == 0:
                        dve.wait(t, *over, attention_over[0])
                        r = dve.do(lambda e, bk=bk, dst=dst: nc.vector.tensor_copy(dst, bank[bk][:, :]), e_acc)
                    elif g < NG - 1:
                        dve.wait(t, *acc_ready[tile, h])
                        r = dve.do(lambda e, bk=bk, dst=dst: nc.vector.tensor_tensor(dst, bank[bk][:, :], dst, ALU.add), e_acc)
                    else:
                        d, d_ready = ds[0]
                        y = last_page[tile % 2][0]
                        dve.wait(t, d_ready, *last_page[tile % 2][1])
                        r = dve.do(lambda e, bk=bk, y=y, d=d, cols=cols: nc.vector.tensor_tensor(
                            page[y][:, cols], bank[bk][:, :], page[d][:, cols], ALU.mult), e_acc)
                    readers[bk] = (r,)
                    acc_ready[tile, h] = (r,)
                    yield 8 * 216, 0
                if g == NG - 2:
                    yield from prepare(tile)
                if g == NG - 1:
                    order.after(200, lambda tile=tile, r=r: finish(tile, r))
            hid_readers[slot] = (t,)
            if tb == B - 1:
                down_last[g] = t

        gu_last, down_last = {}, {}
        ds = [None]
        prepared, last_page = {}, []

        def prepare(tile):
            if ds[0] is None:
                d, arrived = load_page(down_s.partition_broadcast(P), lambda pg: pg[:, :])
                dve.wait(arrived)
                t = dve.do(lambda e: nc.vector.tensor_scalar(page[d][:, :], page[d][:, :], sc[:, 5:6], None, ALU.mult), e_fin)
                ds[0] = (d, t)
            while not free_pages:
                yield BLOCKED
            d, d_ready = ds[0]
            i, before = take_page()
            arrived = load(page[i][:, :], x1_dram[tile], page_ev[i], sp, waits=(x1_stored[tile], *before))
            row = acc[:, tile, :]
            pool.wait(*acc_ready[tile, 0], *acc_ready[tile, 1], d_ready, pool_last[0])
            t = pool_last[0] = pool.do(lambda e: nc.gpsimd.tensor_tensor(row, row, page[d][:, :], ALU.mult), e_finpool)
            to_add.append((tile, i, t, arrived))
            if len(to_add) > 1:
                add_x1()

        to_add = []

        def add_x1():
            tile, i, t, arrived = to_add.pop(0)
            row = acc[:, tile, :]
            dve.wait(t, arrived)
            t = dve.do(lambda e: nc.vector.tensor_tensor(row, row, page[i][:, :], ALU.add), e_fin)
            give_page(i, t)
            prepared[tile] = t

        def finish(tile, r):
            y = last_page[tile % 2][0]
            row = acc[:, tile, :]
            dve.wait(r, prepared[tile])
            t = dve.do(lambda e: nc.vector.tensor_tensor(row, row, page[y][:, :], ALU.add), e_fin)
            last_page[tile % 2] = (y, (t,))

            def store(n):
                sp.wait(n)
                sp.do(lambda e: e.dma_start(out[tile], row), e_out, 16)

            order.after(0, lambda: layernorm(row, tile % 2, t, store))

        e_finpool = ev("final_pool")
        e_out = ev("out_dma")
        NG = FC // GC

        def group_weights(g, kinds, last):
            for c in range(g * GC, min((g + 1) * GC, FC)):
                free = over
                if c >= NW:
                    while (c - NW) // GC not in last:
                        yield BLOCKED
                    free = (last[(c - NW) // GC],)
                yield from weights(c, kinds, free)

        def gate_up_weights(g):
            return group_weights(g, (0, 1), gu_last)

        def down_weights(g):
            return group_weights(g, (2,), down_last)

        def last_output():
            yield from output(B - 1)
            attention_over.append((e_proj, e_proj.count))

        def ffn():
            yield from gate_up_weights(0)
            loads = down_weights(0)
            pending = None
            for g in range(NG):
                for tb in range(B):
                    slot = (g * B + tb) % 2
                    ready = []
                    while tb not in x1T_ready or x1T_ready[tb][1] < NT * 16:
                        yield BLOCKED
                    for said in gate_up(g, tb, slot, ready):
                        next(loads, None)
                        yield said
                    if pending:
                        if pending[1] == 0:
                            yield from loads
                            loads = gate_up_weights(pending[0] + 1)
                        while not attention_over:
                            yield BLOCKED
                        for said in down(*pending):
                            next(loads, None)
                            yield said
                    pending = (g, tb, slot, ready)
                yield from loads
                loads = down_weights(g + 1)
            yield from down(*pending)

        attention_over = []
        order.run([last_output(), ffn(), load_x1T()])
        sp.wait((e_out, e_out.count))

        with nc.Block() as block:
            block.tensor(pe.run)
            block.scalar(act.run)
            block.vector(dve.run)
            block.gpsimd(pool.run)
            block.sync(sp.run)


def rope_tables():
    freqs = (np.float32(1.0) / np.float32(THETA) ** (np.arange(0, HD, 2, dtype=np.float32) / np.float32(HD))).astype(np.float32)
    ang = np.outer(np.arange(S, dtype=np.float32), freqs).astype(np.float32).astype(np.float64)
    cos, sin = np.cos(ang), np.sin(ang)
    c, s = np.concatenate([cos, cos], 1), np.concatenate([-sin, sin], 1)
    k = PROJ_DOWN * QK_UP
    q = k / np.sqrt(HD)
    t = np.stack([c * q, s * q, c * k, s * k], 1).astype(np.float32)
    return np.ascontiguousarray(t.reshape(NT, P, 4, HD).transpose(1, 0, 2, 3))


def causal_mask():
    i = np.arange(P)
    m = np.zeros((P, S), np.float32)
    m[:, S - P:] = np.where(i[None, :] > i[:, None], MASKED, 0.0)
    return m


def kernel(**inputs):
    import concourse.bacc as bacc
    from concourse.bass_utils import run_bass_kernel_spmd

    g = {k.replace("L0_", ""): np.asarray(v) for k, v in inputs.items()}
    bf16, f16 = mybir.dt.np(BF16), np.float16
    even_odd = np.concatenate([np.arange(0, HD, 2), np.arange(1, HD, 2)])

    def heads_split(w, n):
        return w.reshape(D, n, HD)[:, :, even_odd].reshape(D, n * HD)

    def chunked(w):
        return w.reshape(KD, P, -1).transpose(1, 0, 2)

    x = g["attn_x"]
    causal = causal_mask()
    arrays = {
        "xT": x.reshape(B, S, KD, P).transpose(0, 3, 2, 1),
        "x": x.reshape(TILES, P, D),
        "wq": chunked(heads_split(g["attn_wq"], NH)),
        "wkv": chunked(np.concatenate([heads_split(g["attn_wk"], NKV), g["attn_wv"]], 1)),
        "wo": chunked(g["attn_wo"]),
        "gateT": g["ffn_gate_t"].reshape(FC, P, KD, P).transpose(0, 3, 2, 1).reshape(FC, P, D),
        "upT": g["ffn_up_t"].reshape(FC, P, KD, P).transpose(0, 3, 2, 1).reshape(FC, P, D),
        "downT": g["ffn_down_t"].T.reshape(FC, P, D),
        "gate_s": g["ffn_gate_s"].reshape(FC, P).T,
        "up_s": g["ffn_up_s"].reshape(FC, P).T,
        "down_s": g["ffn_down_s"],
        "rope": rope_tables(),
        "causal": causal.astype(bf16),
        "identH": np.eye(P).astype(f16),
    }
    arrays = {k: np.ascontiguousarray(v) for k, v in arrays.items()}
    nc = bacc.Bacc("TRN2", target_bir_lowering=False, num_devices=1)
    args = {k: nc.dram_tensor(k, v.shape, mybir.dt.from_np(v.dtype), kind="ExternalInput").ap() for k, v in arrays.items()}
    out = nc.dram_tensor("out", [TILES, P, D], F32, kind="ExternalOutput").ap()
    block_kernel(nc, **args, out=out)
    got = run_bass_kernel_spmd(nc, [arrays], core_ids=[0]).results[0]["out"]
    return np.asarray(got).reshape(B, S, D)
```

```python
import itertools
from contextlib import ExitStack

import numpy as np
import concourse.bass as bass
from concourse import mybir
from concourse.alu_op_type import AluOpType as ALU

F32, F16, BF16, I32 = mybir.dt.float32, mybir.dt.float16, mybir.dt.bfloat16, mybir.dt.int32
ACT = mybir.ActivationFunctionType

P = 128
B, S, D = 4, 512, 1024
NH, NKV, HD = 32, 8, 32
REP = NH // NKV
FF = 3584
KD = D // P
NT = S // P
TILES = B * NT
HALF = 512
UH = 8
UNITS = NH // UH
UG = UH // REP
FC = FF // P
GC = 4
EPS = 1e-5
THETA = 10000.0

STK = 3 * HD
STKM = STK + 2

X_UP, W_UP = 2.0 ** 6, 2.0 ** 8
PROJ_DOWN = 1.0 / (X_UP * W_UP)
QK_UP = 2.0 ** 4
ATT_UP = 2.0 ** 6
OUT_DOWN = 1.0 / (ATT_UP * W_UP)
SCORE_DOWN = 1.0 / QK_UP ** 2
MAX_ONE = QK_UP ** 2
X1_UP = 2.0 ** 10
HID_BOUND = float(D) ** 2 / 2.0 ** 15
MASKED = -1.0e30


class Event:

    def __init__(self, sem):
        self.sem, self.count, self.time = sem, 0, 0.0

    def so_far(self):
        return self, self.count, self.time


def when(*tickets):
    return max((t[2] for t in tickets if t), default=0.0)


class Queue:

    def __init__(self, column, fixed, notice):
        self.todo, self.seen = [], {}
        self.column, self.fixed, self.notice = column, fixed, notice
        self.free = self.need = 0.0

    def wait(self, *tickets):
        self.need = max(self.need, when(*tickets))
        for t in tickets:
            if t is None:
                continue
            event, count, _ = t
            if self.seen.get(id(event), 0) < count:
                self.seen[id(event)] = count
                self.todo.append(lambda e, s=event.sem, c=count: e.wait_ge(s, c))

    def do(self, make, event=None, cols=0, by=1):
        self.free = max(self.free, self.need) + cols * self.column + self.fixed
        self.need = 0.0
        if event is None:
            self.todo.append(lambda e, m=make: m(e))
            return None
        event.count += by
        event.time = self.free + self.notice
        self.todo.append(lambda e, m=make, s=event.sem, n=by: m(e).then_inc(s, n))
        return event.so_far()

    def run(self, e):
        for step in self.todo:
            step(e)


class Order:

    def __init__(self, pe):
        self.pe, self.later, self.n = pe, [], 0
        self.progress = {}

    def after(self, tickets, stage, delay=0.0):
        self.set_down(when(*tickets) + delay, stage)

    def set_down(self, time, stage):
        self.n += 1
        self.later.append((time, self.n, stage))

    def follow_up(self):
        due = min(self.later, key=lambda f: f[:2])
        self.later.remove(due)
        now = max(self.pe.free, due[0])
        said = due[2]()
        if said is BLOCKED:
            self.set_down(now + 200, due[2])
        elif said is not None:
            self.set_down(max(said, now + 1), due[2])
        return said is None

    def run(self, streams, until=None, by_progress=True):
        waiting = [[s, 0.0, s.__name__] for s in streams]
        blocked = 0
        while waiting or self.later:
            if until is not None and until():
                return
            now = self.pe.free
            due = min((f[0] for f in self.later), default=None)
            if due is not None and due <= now:
                blocked = 0 if self.follow_up() else blocked + 1
            else:
                for w in sorted(waiting, key=lambda w: (w[1] > now and w[1], by_progress and self.progress.get(w[2], 0))):
                    if due is not None and w[1] > max(due, now):
                        continue
                    said = next(w[0], None)
                    if said is BLOCKED:
                        continue
                    if said is None:
                        waiting.remove(w)
                    else:
                        w[1] = said
                    blocked = 0
                    break
                else:
                    blocked += 1
                    if due is None:
                        raise RuntimeError("every stream is blocked")
                    if self.follow_up():
                        blocked = 0
            if blocked > 5000:
                raise RuntimeError("no stage can go on")


BLOCKED = "blocked"
PREFETCH_LEAVES = 4
DOWN_STEPS = 4
LEAD = [0, .3, 0]


def block_kernel(nc, xT, x, wq, wkv, wo, gateT, upT, downT, gate_s, up_s, down_s,
                 rope, causal, identH, out):
    x1_dram = nc.dram_tensor("x1_spill", [TILES, P, D], F32, kind="Internal").ap()
    att_dram = nc.dram_tensor("att_spill", [B, NT, P, 2, KD, P], F16, kind="Internal").ap()
    x1T_dram = nc.dram_tensor("x1T_spill", [TILES, P, 2 * KD * P], F16, kind="Internal").ap()

    ctx = ExitStack()
    with ctx:
        pe, act, dve, pool = Queue(1 / 2.4, 3, 200), Queue(1 / 1.2, 100, 170), Queue(1 / 0.96, 70, 160), Queue(2.3, 100, 80)
        sp = Queue(0, 50, 0)
        wire = [0.0]

        def ev(name):
            return Event(ctx.enter_context(nc.semaphore(name)))

        def psum(name, dt=F32, cols=HALF):
            return ctx.enter_context(nc.psum_tensor(name, [P, cols], dt))

        def sb(where, name, shape, dt):
            return where.enter_context(nc.sbuf_tensor(name, [P, *shape], dt))

        bank = [psum(f"bank{i}") for i in range(8)]

        KEPT = 5
        page = [sb(ctx, f"page{i}", [D], F32) for i in range(KEPT)]
        idH = sb(ctx, "idH", [P], F16)
        stats = sb(ctx, "stats", [2, 2, 6], F32)
        mv = sb(ctx, "mv", [2, 2], F32)
        rstd = sb(ctx, "rstd", [2, 3], F32)
        sg = sb(ctx, "gate_scale", [FC], F32)
        su = sb(ctx, "up_scale", [FC], F32)
        sc = sb(ctx, "scale_bounds", [8], F32)

        NPAGE = 8
        A = ctx.enter_context(ExitStack())
        page_ev = [ev(f"page{i}_dma") for i in range(NPAGE)]
        free_pages = [(i, ()) for i in range(NPAGE)]
        page_users = {i: () for i in range(KEPT, NPAGE)}
        retired = []

        def take_page():
            return free_pages.pop(0)

        def give_page(i, *tickets):
            if retired and i >= KEPT:
                page_users[i] = tickets
                retired.append(i)
            else:
                free_pages.append((i, tickets))

        def load(dst, src, event, queue=None, waits=(), size=4 * P * D):
            q = queue or sp
            q.wait(*waits)
            event, count, start = q.do(lambda e: e.dma_start(dst, src), event, by=16)
            wire[0] = max(wire[0], start) + size / 350
            event.time = wire[0] + 1900
            return event.so_far()

        def load_page(src, view):
            i, before = take_page()
            return i, load(view(page[i]), src, page_ev[i], waits=before)

        order = Order(pe)

        e_ln, e_lnpool = ev("ln_step"), ev("ln_newton")
        pool_last = [None]
        ln_last = [(), ()]

        def layernorm(row, slot, ready, then):
            if ln_last[slot] is None:
                return BLOCKED
            before, ln_last[slot] = ln_last[slot], None
            dve.wait(ready, *before)
            for h in range(2):
                t = dve.do(lambda e, h=h: nc.vector.bn_stats(stats[:, slot, h, :], row[:, h * HALF:(h + 1) * HALF]), e_ln, HALF)
            dve.wait(t)
            t = dve.do(lambda e: nc.vector.bn_aggr(mv[:, slot, :], stats[:, slot, :, :]), e_ln)
            v, r, w = rstd[:, slot, 0:1], rstd[:, slot, 1:2], rstd[:, slot, 2:3]
            dve.wait(t)
            t = dve.do(lambda e: nc.vector.tensor_scalar(v, mv[:, slot, 1:2], EPS, None, ALU.add), e_ln)
            dve.wait(t)
            t = dve.do(lambda e: nc.vector.tensor_scalar(r.bitcast(I32), v.bitcast(I32), -0.5, float(0x5F3759DF),
                                                         ALU.mult, ALU.add), e_ln)
            pool.wait(t, pool_last[0])
            for _ in range(3):
                for step in (lambda e: nc.gpsimd.tensor_tensor(w, r, r, ALU.mult),
                             lambda e: nc.gpsimd.tensor_tensor(w, w, v, ALU.mult),
                             lambda e: nc.gpsimd.tensor_scalar(w, w, -0.5, 1.5, ALU.mult, ALU.add),
                             lambda e: nc.gpsimd.tensor_tensor(r, r, w, ALU.mult)):
                    t = pool_last[0] = pool.do(step, e_lnpool, 30)
                    pool.wait(t)

            def rest():
                dve.wait(t)
                n = dve.do(lambda e: nc.vector.tensor_scalar(row, row, mv[:, slot, 0:1], r,
                                                             ALU.subtract, ALU.mult), e_ln, 0.6 * D)
                ln_last[slot] = (n,)
                order.after([n], lambda: then(n))

            order.after([t], rest)

        wq_p = sb(A, "wq_parts", [2, KD, D], F16)
        wkv_p = sb(A, "wkv_parts", [2, KD, 2 * NKV * HD], F16)
        xT_p = sb(A, "xT_parts", [2, KD, S], F16)
        QS = 3
        qT = sb(A, "q_stack", [QS, UH, S], F16)
        kT = sb(A, "k_stack", [2, NKV, S], F16)
        v32 = sb(A, "v32", [2, NT, NKV * HD], F32)
        NNAT = 3
        nat = sb(A, "stack_rows", [NNAT, UH, STK], F16)
        ropeA = sb(A, "rope_cos", [NNAT, UH * HD], F32)
        ropeB = sb(A, "rope_sin", [NNAT, UH * HD], F32)
        NP32 = 8
        p32 = sb(A, "p32", [NP32, S], F32)
        tab = sb(A, "rope_tab", [NT, 4, HD], F32)
        cmask = sb(A, "cmask", [S], BF16)
        ones = sb(A, "ones", [HD], F32)
        mx = sb(A, "row_max", [2, NT, UH], F32)
        mneg = sb(A, "neg_max", [NT, UH], F32)
        m_p = sb(A, "max_parts", [NT, 2, UH], F16)
        mT = sb(A, "max_rows", [S], F16)

        wo_p = sb(A, "wo_parts", [2, KD, D], F16)
        page += [sb(A, f"page{i}", [D], F32) for i in range(KEPT, NPAGE)]

        A.close()
        BB = ctx.enter_context(ExitStack())
        x1T = sb(BB, "x1T", [TILES, 2, KD, P], F16)
        NW = 6
        w_gate = sb(BB, "w_gate", [NW, KD, P], F16)
        w_up = sb(BB, "w_up", [NW, KD, P], F16)
        w_down = sb(BB, "w_down", [NW, D], F16)
        hid = sb(BB, "hid", [2, GC, 2, S], F16)
        silu = sb(BB, "silu", [2, S], F32)
        bias = sb(BB, "bias", [2, 1], F32)
        acc = sb(BB, "acc", [TILES, D], F32)

        e_const, e_const2 = ev("const_dma"), ev("const_set")
        consts = None
        for dst, src in ((idH[:, :], identH), (cmask[:, :], causal),
                         (tab[:, :, :, :], rope)):
            consts = load(dst, src, e_const, act)
        pool.wait(pool.do(lambda e: nc.gpsimd.memset(ones[:, :], 1.0), e_const2))
        const_set = pool_last[0] = pool.do(lambda e: nc.gpsimd.memset(kT[96:128, :, :, :], MAX_ONE), e_const2)

        e_sc, e_sdma = ev("scales"), ev("scale_dma")
        load(sg[:, :], gate_s, e_sdma, act, size=P * FC * 4)
        s_in = load(su[:, :], up_s, e_sdma, act, size=P * FC * 4)
        RMAX = bass.bass_isa.ReduceOp.max
        scales = []

        def bound_hidden():
            dve.wait(s_in)
            dve.do(lambda e: nc.vector.tensor_reduce(sc[:, 0:1], sg[:, :], mybir.AxisListType.X, ALU.max,
                                                     apply_absolute_value=True))
            t = dve.do(lambda e: nc.vector.tensor_reduce(sc[:, 1:2], su[:, :], mybir.AxisListType.X, ALU.max,
                                                         apply_absolute_value=True), e_sc)
            pool.wait(t, pool_last[0])
            t = pool_last[0] = pool.do(lambda e: nc.gpsimd.partition_all_reduce(sc[:, 2:4], sc[:, 0:2], P, RMAX), e_sc)
            dve.wait(t)
            t = dve.do(lambda e: nc.vector.tensor_scalar(sc[:, 4:5], sc[:, 2:3], sc[:, 3:4], HID_BOUND, ALU.mult, ALU.mult), e_sc)
            dve.wait(t)
            t = dve.do(lambda e: nc.vector.tensor_scalar(sc[:, 5:6], sc[:, 4:5], 1e-30, None, ALU.max), e_sc)
            dve.wait(t)
            t = dve.do(lambda e: nc.vector.reciprocal(sc[:, 6:7], sc[:, 5:6]), e_sc)
            dve.wait(t)
            dve.do(lambda e: nc.vector.tensor_scalar(sg[:, :], sg[:, :], 1.0 / X1_UP, None, ALU.mult))
            scales.append(dve.do(lambda e: nc.vector.tensor_scalar(su[:, :], su[:, :], sc[:, 6:7], 1.0 / X1_UP, ALU.mult, ALU.mult), e_sc))

        order.set_down(60e3, bound_hidden)

        e_hi, e_lo = ev("split_hi"), ev("split_lo")

        def split_page(i, arrived, hi, lo, up, ready, keys, before=()):
            src = page[i][:, :]

            def split_hi():
                act.wait(arrived, *before)
                h = act.do(lambda e: nc.scalar.activation(hi, src, ACT.Copy, scale=up), e_hi, D)

                def split_lo():
                    dve.wait(arrived, h, *before)
                    l = dve.do(lambda e: nc.vector.scalar_tensor_tensor(lo, src, up, hi, ALU.mult, ALU.subtract), e_lo, D)
                    give_page(i, h, l)
                    ready.update((key, l) for key in keys)

                order.after([h], split_lo)

            order.after([arrived], split_hi)

        def flat(ap):
            return ap.rearrange("p a b -> p (a b)")

        xT_ready = {}
        xT_free = [()]

        def load_pair(w, k, parts, up, ready, keys, before=()):
            while not free_pages:
                yield BLOCKED
            i, t = load_page(w[:, k:k + 2, :], lambda pg: pg[:, :].rearrange("p (a b) -> p a b", a=2))
            split_page(i, t, flat(parts[:, 0, k:k + 2, :]), flat(parts[:, 1, k:k + 2, :]), up, ready, keys, before)
            yield pe.free

        def load_x(b, k):
            return load_pair(xT[b], k, xT_p, X_UP, xT_ready, [(b, k), (b, k + 1)], xT_free[0])

        wkv_ready, wq_ready, wo_ready = {}, {}, {}

        def load_square(w, parts, ready, gap):
            for k in range(KD):
                while not free_pages:
                    yield BLOCKED
                i, t = load_page(w[:, k, :], lambda pg: pg[:, :])
                split_page(i, t, parts[:, 0, k, :], parts[:, 1, k, :], W_UP, ready, [k])
                yield pe.free + gap

        def first_loads():
            for k in range(0, KD, 2):
                yield from load_x(0, k)
                yield from load_pair(wkv, k, wkv_p, W_UP, wkv_ready, [k, k + 1])
            yield from load_square(wq, wq_p, wq_ready, 0)
            yield from load_square(wo, wo_p, wo_ready, 1200)

        TCOLS = 150

        readers = {i: () for i in range(8)}
        PROJ, TRANS, SCORE, PV, DEN = (0, 1), (2,), (3, 4, 5), 6, 7

        def next_bank(ring):
            return min((i for i in ring if readers[i] is not None), key=lambda i: when(*readers[i]), default=None)

        def free_bank(ring, *tickets):
            waited = None
            while True:
                i = next_bank(ring)
                if i is None:
                    yield BLOCKED
                elif waited == i:
                    return
                else:
                    waited = i
                    yield when(*readers[i], *tickets)

        e_proj, e_rope, e_ropep, e_nathi, e_natlo = ev("proj"), ev("rope"), ev("rope_sum"), ev("nat_hi"), ev("nat_lo")
        e_tr, e_trc = ev("transposed"), ev("stack_copied")
        nat_turn = [0]
        nat_readers = [()] * NNAT
        rope_readers = [()] * NNAT

        def three_passes(dst, lhs, rhs, ready, cols):
            for k in range(KD):
                while None in ready(k):
                    yield BLOCKED
                yield when(*ready(k))
                pe.wait(*ready(k))
                for n, (a, c) in enumerate(((0, 0), (0, 1), (1, 0))):
                    first, last = k == 0 and n == 0, k == KD - 1 and n == 2
                    t = pe.do(lambda e, left=lhs(a, k), right=rhs(c, k), first=first, last=last:
                              nc.tensor.matmul(dst, left, right, start=first, stop=last), e_proj if last else None, cols)
            return t

        def rotate(bk, nh, t, kind, ready, then):
            s = nat_turn[0] % NNAT
            if nat_readers[s] is None:
                return BLOCKED
            nat_turn[0] += 1
            before_nat, nat_readers[s] = nat_readers[s], None
            src = bank[bk][:, 0:nh * HD].rearrange("p (h c) -> p h c", h=nh)
            ta = ropeA[:, s, 0:nh * HD].rearrange("p (h c) -> p h c", h=nh)
            tb = ropeB[:, s, 0:nh * HD].rearrange("p (h c) -> p h c", h=nh)
            q = HD // 2

            def tabled(n, lo, hi):
                return tab[:, t:t + 1, 2 * kind + n, lo:hi].broadcast_to([P, nh, hi - lo])

            dve.wait(ready, consts, *rope_readers[s])
            dve.do(lambda e: nc.vector.tensor_tensor(ta, src, tabled(0, 0, HD), ALU.mult), cols=nh * HD)
            dve.do(lambda e: nc.vector.tensor_tensor(tb[:, :, 0:q], src[:, :, q:HD], tabled(1, 0, q), ALU.mult), cols=nh * q)
            r = dve.do(lambda e: nc.vector.tensor_tensor(tb[:, :, q:HD], src[:, :, 0:q], tabled(1, q, HD), ALU.mult), e_rope, nh * q)
            readers[bk] = (r,)
            pool.wait(r, pool_last[0])
            r = pool_last[0] = pool.do(lambda e: nc.gpsimd.tensor_tensor(
                ropeA[:, s, 0:nh * HD], ropeA[:, s, 0:nh * HD], ropeB[:, s, 0:nh * HD], ALU.add), e_ropep, nh * HD)
            rows = nat[:, s, 0:nh, :].rearrange("p h (f c) -> p h f c", f=3)
            field = (slice(0, 3, 2), 1) if kind else (slice(0, 2), 2)

            def split_hi():
                act.wait(r, *before_nat)
                h = act.do(lambda e: nc.scalar.activation(
                    rows[:, :, field[0], :], ta.unsqueeze(2).broadcast_to([P, nh, 2, HD]), ACT.Copy), e_nathi, 2 * nh * HD)

                def split_lo():
                    dve.wait(r, h)
                    l = dve.do(lambda e: nc.vector.tensor_tensor(rows[:, :, field[1], :], ta, rows[:, :, 0, :],
                                                                 ALU.subtract), e_natlo, nh * HD)
                    rope_readers[s] = (h, l)
                    order.after([l], lambda: then(s, l))

                order.after([h], split_lo)

            order.after([r], split_hi)

        def transpose_heads(s, nh, ready, dst, before):
            tb = bank[TRANS[0]][:, :].bitcast(F16).rearrange("p (h c) -> p h c", h=8)
            pe.wait(ready, consts, *readers[TRANS[0]])
            for h in range(nh):
                t = pe.do(lambda e, h=h: nc.tensor.transpose(tb[0:STK, h, :], nat[:, s, h, :], idH[:, :]),
                          e_tr if h == nh - 1 else None, TCOLS)
            nat_readers[s] = (t,)
            dve.wait(t, *before)
            c = dve.do(lambda e: nc.vector.tensor_copy(dst, tb[0:STK, 0:nh, :]), e_trc, HALF)
            readers[TRANS[0]] = (c,)
            return c

        k_ready, v_ready, q_ready = {}, {}, {}
        st_done = {}
        pv_done = {}
        e_v = ev("v")

        def project(u, with_kv):
            b, g = divmod(u, UNITS)
            while u >= QS and u - QS not in attended:
                yield BLOCKED
            steps = ([("kv", t) for t in range(NT)] if with_kv else []) + [("q", t) for t in range(NT)]
            for what, t in steps:
                yield from free_bank(PROJ)
                bk = next_bank(PROJ)
                order.progress["projections"] = u - 1 + (steps.index((what, t)) / len(steps)) + LEAD[1]
                pe.wait(*readers[bk])
                readers[bk] = None
                rows = slice(t * P, (t + 1) * P)
                if what == "kv":
                    done = yield from three_passes(bank[bk][:, :], lambda a, k: xT_p[:, a, k, rows],
                                        lambda c, k: wkv_p[:, c, k, :], lambda k: (xT_ready.get((b, k)), wkv_ready.get(k)), HALF)
                    nh, record, key = NKV, k_ready, (b, t)
                    dst, before = kT[0:STK, b % 2, :, rows], (b - 1) * UNITS - 1
                else:
                    done = yield from three_passes(bank[bk][:, 0:UH * HD], lambda a, k: xT_p[:, a, k, rows],
                                        lambda c, k: wq_p[:, c, k, g * UH * HD:(g + 1) * UH * HD],
                                        lambda k: (xT_ready.get((b, k)), wq_ready.get(k)), UH * HD)
                    nh, record, key = UH, q_ready, (u, t)
                    dst, before = qT[0:STK, u % QS, :, rows], u - QS
                    if t == NT - 1 and g == UNITS - 1:
                        xT_free[0] = (done,)

                def transpose(s, ready, nh=nh, dst=dst, before=before, record=record, key=key):
                    if when(*readers[TRANS[0]]) > pe.free:
                        return when(*readers[TRANS[0]])
                    record[key] = transpose_heads(s, nh, ready, dst, [st_done.get(before)])

                def receive(what=what, t=t, bk=bk, done=done, nh=nh, transpose=transpose):
                    if what == "q":
                        return rotate(bk, nh, t, 0, done, transpose)
                    nk = NKV * HD
                    act.wait(done, pv_done.get((b - 1) * UNITS - 1))
                    vt = v32[:, b % 2, t, :]
                    h = v_ready[b, t] = act.do(lambda e: nc.scalar.activation(
                        vt, bank[bk][:, nk:2 * nk], ACT.Copy, scale=PROJ_DOWN), e_v, nk)
                    order.after([h], lambda: rotate(bk, nh, t, 1, h, transpose))

                order.after([done], receive)

        e_smax, e_mx, e_mpart, e_mtr, e_mcopy = ev("score_q"), ev("row_max"), ev("max_part"), ev("max_tr"), ev("max_copy")
        e_mrow = [ev("max_rows_dma0"), ev("max_rows_dma1")]
        m_ready, m_there = {}, set()

        def maxima(u):
            b, g = divmod(u, UNITS)
            for i in range(NT):
                n = (i + 1) * P
                while (u, i) not in q_ready or (b, i) not in k_ready:
                    yield BLOCKED
                for h in range(UH):
                    kv = (g * UH + h) // REP
                    order.progress["all_maxima"] = u - 1 + (0, .1, .3, .6)[i] + (.1, .2, .3, .4)[i] * h / UH + LEAD[0]
                    yield from free_bank(SCORE, q_ready[u, i], k_ready[b, i])
                    bk = next_bank(SCORE)
                    pe.wait(q_ready[u, i], k_ready[b, i], *readers[bk])
                    t = pe.do(lambda e, bk=bk, h=h, kv=kv, i=i, n=n: nc.tensor.matmul(
                        bank[bk][:, 0:n], qT[0:STK, u % QS, h, i * P:n], kT[0:STK, b % 2, kv, 0:n],
                        start=True, stop=True), e_smax, n)
                    dve.wait(t)
                    r = dve.do(lambda e, bk=bk, h=h, i=i, n=n: nc.vector.tensor_tensor_reduce(
                        out=bank[bk][:, 0:n], in0=bank[bk][:, 0:n], in1=cmask[:, S - n:S], scale=1.0, scalar=MASKED,
                        op0=ALU.add, op1=ALU.max, accum_out=mx[:, u % 2, i, h:h + 1]), e_mx, n)
                    readers[bk] = (r,)
            dve.wait(r, m_ready.get(("tr", u - 1)))
            mm = mx[:, u % 2, :, :]
            a = dve.do(lambda e: nc.vector.tensor_scalar(mneg[:, :, :], mm, -1.0 / MAX_ONE, None, ALU.mult), e_mpart, NT * UH)
            dve.wait(a)
            a = dve.do(lambda e: nc.vector.tensor_copy(m_p[:, :, 0, :], mneg[:, :, :]), e_mpart, NT * UH)
            dve.wait(a)
            a = dve.do(lambda e: nc.vector.tensor_tensor(m_p[:, :, 1, :], mneg[:, :, :], m_p[:, :, 0, :], ALU.subtract), e_mpart, NT * UH)

            def transpose():
                tb = bank[TRANS[0]][:, :].bitcast(F16)
                if when(*readers[TRANS[0]]) > pe.free:
                    return when(*readers[TRANS[0]])
                pe.wait(a, *readers[TRANS[0]])
                for i in range(NT):
                    t = pe.do(lambda e, i=i: nc.tensor.transpose(tb[0:2 * UH, i * P:(i + 1) * P],
                                                                 m_p[:, i, :, :].rearrange("p a h -> p (a h)"), idH[:, :]),
                              e_mtr if i == NT - 1 else None, TCOLS)
                m_ready["tr", u] = t
                dve.wait(t, *m_ready.get(("dma", u - 1), ()))
                c = dve.do(lambda e: nc.vector.tensor_copy(mT[0:2 * UH, :], tb[0:2 * UH, 0:S]), e_mcopy, 0.5 * S)
                readers[TRANS[0]] = (c,)
                both = []
                for n in range(2):
                    both.append(load(qT[STK + n:STK + n + 1, u % QS, :, :], mT[n * UH:(n + 1) * UH, :], e_mrow[n], sp,
                                     waits=(c, st_done.get(u - QS)), size=UH * S * 2))
                m_ready["dma", u] = m_ready[u] = tuple(both)
                m_there.add(u)

            order.after([a], transpose)
            yield pe.free

        e_st, e_exp, e_causal, e_pv, e_den = ev("score_k"), ev("exp"), ev("causal"), ev("pv"), ev("den")
        e_take, e_rden, e_att, e_atthi, e_attlo = ev("pv_taken"), ev("rden"), ev("att"), ev("att_hi"), ev("att_lo")
        p32_readers = [()] * NP32
        p_turn = [0]
        att_ready = {}

        def attend(u):
            b, g = divmod(u, UNITS)

            def pv(G, j, slots, ready):
                lo = j * P
                kv = g * UG + G
                pe.wait(v_ready[b, j], const_set, *ready)
                if j == 0:
                    pe.wait(*readers[PV], *readers[DEN])
                for dst, lhs, event in ((PV, v32[:, b % 2, j, kv * HD:(kv + 1) * HD], e_pv), (DEN, ones[:, :], e_den)):
                    for hh in range(REP):
                        t = pe.do(lambda e, dst=dst, hh=hh, lhs=lhs, sl=slots[hh]: nc.tensor.matmul(
                            bank[dst][hh * HD:(hh + 1) * HD, lo:S], lhs, p32[:, sl, lo:S], start=j == 0,
                            stop=j == NT - 1, tile_position=(0, hh * HD)), event if hh == REP - 1 else None,
                            1.08 * (S - lo))
                for s in slots:
                    p32_readers[s] = (t,)
                pv_done[u] = t
                if j == NT - 1:
                    readers[PV] = readers[DEN] = None
                    order.after([t], lambda: normalise(G, t))

            def normalise(G, done):
                gg = g * UG + G
                if not free_pages:
                    return BLOCKED
                i, before = take_page()
                den, pvs = page[i][:, 0:S], page[i][:, S:2 * S]
                act.wait(done, *before)
                d = act.do(lambda e: nc.scalar.activation(den, bank[DEN][:, :], ACT.Copy), e_take, S)
                a = act.do(lambda e: nc.scalar.activation(pvs, bank[PV][:, :], ACT.Copy, scale=ATT_UP), e_take, S)
                readers[PV] = readers[DEN] = (a,)

                def invert(c):
                    q = den[:, c * P:(c + 1) * P]
                    dve.wait(d)
                    r = dve.do(lambda e: nc.vector.reciprocal(q, q), e_rden, 6 * P)
                    order.after([r], (lambda: invert(c + 1)) if c < NT - 1 else (lambda: multiply(r)))

                def multiply(r):
                    dve.wait(r, a)
                    m = dve.do(lambda e: nc.vector.tensor_tensor(pvs, pvs, den, ALU.mult), e_att, S)
                    parts = den.bitcast(F16)
                    act.wait(m)
                    h = act.do(lambda e: nc.scalar.activation(parts[:, 0:S], pvs, ACT.Copy), e_atthi, S)

                    def split_lo():
                        dve.wait(h)
                        l = dve.do(lambda e: nc.vector.tensor_tensor(parts[:, S:2 * S], pvs, parts[:, 0:S],
                                                                     ALU.subtract), e_attlo, S)
                        for a_ in range(2):
                            stored = load(att_dram[b, :, :, a_, gg, :].rearrange("t p c -> p t c"),
                                          parts[:, a_ * S:(a_ + 1) * S].rearrange("p (t c) -> p t c", t=NT), page_ev[i],
                                          sp, waits=(l,), size=P * S * 2)
                        give_page(i, l, stored)
                        att_ready[b, gg] = stored

                    order.after([h], split_lo)

                order.after([d], lambda: invert(0))

            late = None
            for G in range(UG):
                kv = g * UG + G
                for j in range(NT):
                    lo = j * P
                    slots, ready = [], []
                    for hh in range(REP):
                        h = G * REP + hh
                        while u not in m_there:
                            yield BLOCKED
                        order.progress["attends"] = u + (G + (0, .4, .7, .9)[j] + (.4, .3, .2, .1)[j] * hh / REP) / UG
                        inputs = (*m_ready[u], const_set, *[q_ready[u, i] for i in range(j, NT)], k_ready[b, j])
                        yield from free_bank(SCORE, *inputs)
                        if late and (len(slots) == min(NP32 - REP, REP) - 1 or when(*late[3]) <= pe.free):
                            while late[1] == 0 and readers[PV] is None:
                                yield BLOCKED
                            yield when(*late[3], *(readers[PV] if late[1] == 0 else ()))
                            pv(*late)
                            late = None
                            yield from free_bank(SCORE)
                        bk = next_bank(SCORE)
                        pe.wait(*inputs, *readers[bk])
                        t = pe.do(lambda e, bk=bk, h=h, lo=lo, kv=kv: nc.tensor.matmul(
                            bank[bk][:, 0:S - lo], kT[0:STKM, b % 2, kv, lo:lo + P], qT[0:STKM, u % QS, h, lo:S],
                            start=True, stop=True), e_st, S - lo)
                        st_done[u] = t
                        a = p_turn[0] % NP32
                        p_turn[0] += 1
                        act.wait(t, *p32_readers[a])
                        x_ = act.do(lambda e, bk=bk, a=a, lo=lo: nc.scalar.activation(
                            p32[:, a, lo:S], bank[bk][:, 0:S - lo], ACT.Exp, scale=SCORE_DOWN), e_exp, S - lo)
                        readers[bk] = (x_,)
                        pool.wait(x_, pool_last[0])
                        m_ = pool_last[0] = pool.do(lambda e, a=a, lo=lo: nc.gpsimd.affine_select(
                            out=p32[:, a, lo:lo + P], in_=p32[:, a, lo:lo + P], compare_op=ALU.is_ge, fill=0.0,
                            base=0, pattern=[[1, P]], channel_multiplier=-1), e_causal, 0.6 * P)
                        slots.append(a)
                        ready.append(m_)
                    late = (G, j, slots, ready)
            attended.add(u)
            yield when(*late[3])
            pv(*late)
            yield pe.free

        attended = set()

        e_res, e_x1hi, e_x1lo, e_x1tr, e_x1c = ev("residual"), ev("x1_hi"), ev("x1_lo"), ev("x1_tr"), ev("x1_copy")
        x1_stored, x1T_stored = {}, {}
        sent = []

        def output(b):
            while any((b, gg) not in att_ready for gg in range(KD)):
                yield BLOCKED

            def store_transposed(tile, i, l):
                if not free_pages:
                    return BLOCKED
                o, before = take_page()
                parts = page[i][:, :].bitcast(F16).rearrange("p (a k c) -> p a k c", a=2, k=KD)
                dst = page[o][:, :].bitcast(F16).rearrange("p (a k c) -> p a k c", a=2, k=KD)
                tb = bank[TRANS[0]][:, :].bitcast(F16).rearrange("p (h c) -> p h c", h=KD)

                def part(a):
                    if when(*readers[TRANS[0]]) > pe.free:
                        return when(*readers[TRANS[0]])
                    pe.wait(l, *readers[TRANS[0]])
                    for k in range(KD):
                        t = pe.do(lambda e, k=k: nc.tensor.transpose(tb[:, k, :], parts[:, a, k, :], idH[:, :]),
                                  e_x1tr if k == KD - 1 else None, TCOLS)
                    act.wait(t, *before)
                    c = act.do(lambda e: nc.scalar.activation(dst[:, a, :, :], tb[:, :, :], ACT.Copy), e_x1c, D)
                    readers[TRANS[0]] = (c,)
                    if a == 0:
                        order.after([c], lambda: part(1))
                    else:
                        give_page(i, t)
                        s = load(x1T_dram[tile], page[o][:, :].bitcast(F16), page_ev[o], sp, waits=(c,))
                        x1T_stored[tile] = s
                        give_page(o, s)

                order.after([l], lambda: part(0))

            def split_x1(tile, i, row, n):
                s = load(x1_dram[tile], row, page_ev[i], sp, waits=(n,))
                x1_stored[tile] = s
                o, before = take_page()
                hi, lo = page[o][:, 0:HALF].bitcast(F16), page[o][:, HALF:D].bitcast(F16)
                act.wait(n, *before)
                h = act.do(lambda e: nc.scalar.activation(hi, row, ACT.Copy, scale=X1_UP), e_x1hi, D)

                def split_lo():
                    dve.wait(h, *before)
                    l = dve.do(lambda e: nc.vector.scalar_tensor_tensor(lo, row, X1_UP, hi, ALU.mult, ALU.subtract), e_x1lo, D)
                    give_page(i, s, h, l)
                    order.after([l], lambda: store_transposed(tile, o, l))

                order.after([h], split_lo)

            for t in range(NT):
                while len(free_pages) < 4:
                    yield BLOCKED
                tile = b * NT + t
                at, before = take_page()
                i, arrived = load_page(x[tile], lambda pg: pg[:, :])
                yield when(*before, *[att_ready[b, gg] for gg in range(KD)])
                att = page[at][:, :].bitcast(F16).rearrange("p (a k c) -> p a k c", a=2, k=KD)
                att_there = load(page[at][:, :].bitcast(F16), att_dram[b, t].rearrange("p a k c -> p (a k c)"), page_ev[at],
                                 sp, waits=(*before, *[att_ready[b, gg] for gg in range(KD)]))
                row = page[i][:, :]
                for h in range(2):
                    cols = slice(h * HALF, (h + 1) * HALF)
                    order.progress["outputs"] = (b + 1) * UNITS + UNITS * (2 * t + h) / (2 * NT) + LEAD[2]
                    yield from free_bank(PROJ)
                    bk = next_bank(PROJ)
                    pe.wait(*readers[bk])
                    readers[bk] = None
                    done = yield from three_passes(bank[bk][:, :], lambda a, k: att[:, a, k, :],
                                        lambda c, k: wo_p[:, c, k, cols], lambda k: (att_there, wo_ready.get(k)), HALF)

                    def receive(h=h, bk=bk, done=done, row=row, cols=cols, arrived=arrived, tile=tile, i=i):
                        dve.wait(done, arrived)
                        r = dve.do(lambda e: nc.vector.scalar_tensor_tensor(
                            row[:, cols], bank[bk][:, :], OUT_DOWN, row[:, cols], ALU.mult, ALU.add), e_res, HALF)
                        readers[bk] = (r,)
                        if h:
                            order.after([r], lambda: layernorm(
                                row, tile % 2, r, lambda n: split_x1(tile, i, row, n) if free_pages else BLOCKED))

                    order.after([done], receive)
                give_page(at, done)

        e_x1T = [ev(f"x1T_load{t}") for t in range(B)]
        x1T_ready, projections_over = {}, []
        over, attention_over = [], []

        def load_x1T():
            for t in range(TILES):
                while t not in x1T_stored or not projections_over:
                    yield BLOCKED
                x1T_ready[t // NT] = load(x1T[:, t, :, :, :].rearrange("p a k c -> p (a k c)"), x1T_dram[t],
                                          e_x1T[t // NT], sp, waits=(x1T_stored[t], *projections_over))
                yield pe.free + 3000

        e_w = ev("weights_cast")
        w_ready = {}

        def weights(c, kinds, free):
            for kind in kinds:
                w, dst = ((gateT, w_gate), (upT, w_up), (downT, w_down))[kind]
                while not free_pages or not over and len(free_pages) <= PREFETCH_LEAVES:
                    yield BLOCKED
                i, before = take_page()
                pg = page[i][:, :].bitcast(I32)
                arrived = load(pg, w[c], page_ev[i], sp, waits=before)
                to = dst[:, c % NW, :] if kind == 2 else flat(dst[:, c % NW, :, :])

                def cast(i=i, kind=kind, to=to, pg=pg, arrived=arrived):
                    if not over:
                        return BLOCKED
                    act.wait(arrived, *free)
                    t = act.do(lambda e: nc.scalar.activation(to, pg, ACT.Copy), e_w, D)
                    give_page(i, t)
                    w_ready[c, kind] = t

                order.after([arrived], cast)
                yield pe.free

        GATE, UP, DOWN = (4, 5), (6, 7), (0, 1, 2, 3)
        e_gu, e_silu, e_h, e_hhi, e_hlo = ev("gate_up"), ev("silu"), ev("hidden"), ev("hid_hi"), ev("hid_lo")
        e_down, e_acc, e_fin = ev("down"), ev("acc"), ev("final")
        silu_readers, hid_readers = [over] * 2, [over] * 2
        small = [0]
        acc_ready = {}

        def gate_up(g, tb, slot, c, hid_ready):
            ch = g * GC + c
            w = ch % NW
            gb, ub = next_bank(GATE), next_bank(UP)
            for kind, bk, ws in ((0, gb, w_gate), (1, ub, w_up)):
                while (ch, kind) not in w_ready:
                    yield BLOCKED
                pe.wait(w_ready[ch, kind], x1T_ready[tb], *readers[bk])
                for k in range(KD):
                    for a in range(2):
                        t = pe.do(lambda e, bk=bk, ws=ws, w=w, k=k, a=a: nc.tensor.matmul(
                            bank[bk][:, :], ws[:, w, k, :], x1T[:, tb * NT:(tb + 1) * NT, a, k, :],
                            start=(k == 0 and a == 0), stop=(k == KD - 1 and a == 1)),
                            e_gu if k == KD - 1 and a == 1 else None, S)
                if kind == 0:
                    gt = t
            s = small[0] % 2
            small[0] += 1
            act.wait(gt, *scales, *silu_readers[s])
            x_ = act.do(lambda e, gb=gb, ch=ch, s=s: nc.scalar.activation(silu[:, s, :], bank[gb][:, :], ACT.Silu,
                                                                          scale=sg[:, ch:ch + 1]), e_silu, S)
            readers[gb] = (x_,)
            dve.wait(t, x_)
            h = dve.do(lambda e, ub=ub, ch=ch, s=s: nc.vector.scalar_tensor_tensor(
                silu[:, s, :], bank[ub][:, :], su[:, ch:ch + 1], silu[:, s, :], ALU.mult, ALU.mult), e_h, S)
            readers[ub] = (h,)
            act.wait(h, *hid_readers[slot])
            hi = act.do(lambda e, c=c, s=s: nc.scalar.activation(hid[:, slot, c, 0, :], silu[:, s, :], ACT.Copy), e_hhi, S)
            dve.wait(hi)
            l = dve.do(lambda e, c=c, s=s: nc.vector.tensor_tensor(hid[:, slot, c, 1, :], silu[:, s, :],
                                                                   hid[:, slot, c, 0, :], ALU.subtract), e_hlo, S)
            silu_readers[s] = (hi, l)
            hid_ready.append(l)
            yield pe.free
            if tb == B - 1 and c == GC - 1:
                gu_last[g] = t

        def down(g, tb, slot, hid_ready):
            if g == NG - 1 and tb == 0:
                while to_add:
                    add_x1()
                last_page.extend(take_page() for _ in range(2))
            for i in range(NT):
                tile = tb * NT + i
                for h in range(2):
                    cols = slice(h * HALF, (h + 1) * HALF)
                    bk = next_bank(DOWN)
                    pe.wait(*readers[bk], *hid_ready)
                    for c in range(GC):
                        ch = g * GC + c
                        while (ch, 2) not in w_ready:
                            yield BLOCKED
                        pe.wait(w_ready[ch, 2])
                        for a in range(2):
                            t = pe.do(lambda e, bk=bk, c=c, a=a, i=i, ch=ch, cols=cols: nc.tensor.matmul(
                                bank[bk][:, :], hid[:, slot, c, a, i * P:(i + 1) * P], w_down[:, ch % NW, cols],
                                start=(c == 0 and a == 0), stop=(c == GC - 1 and a == 1)),
                                e_down if c == GC - 1 and a == 1 else None, HALF)
                    dst = acc[:, tile, cols]
                    if g == 0:
                        dve.wait(t, *over, *attention_over)
                        r = dve.do(lambda e, bk=bk, dst=dst: nc.vector.tensor_copy(dst, bank[bk][:, :]), e_acc, HALF)
                    elif g < NG - 1:
                        dve.wait(t, *acc_ready[tile, h])
                        r = dve.do(lambda e, bk=bk, dst=dst: nc.vector.tensor_tensor(dst, bank[bk][:, :], dst, ALU.add), e_acc, HALF)
                    else:
                        d, d_ready = ds[0]
                        while last_page[tile % 2][1] is None:
                            yield BLOCKED
                        y = last_page[tile % 2][0]
                        dve.wait(t, d_ready, *last_page[tile % 2][1])
                        r = dve.do(lambda e, bk=bk, y=y, d=d, cols=cols: nc.vector.tensor_tensor(
                            page[y][:, cols], bank[bk][:, :], page[d][:, cols], ALU.mult), e_acc, HALF)
                    readers[bk] = (r,)
                    acc_ready[tile, h] = (r,)
                    yield pe.free
                if g == NG - 2:
                    yield from prepare(tile)
                if g == NG - 1:
                    last_page[tile % 2] = (y, None)
                    order.after([r], lambda tile=tile, r=r: finish(tile, r))
            hid_readers[slot] = (t,)
            if tb == B - 1:
                down_last[g] = t

        gu_last, down_last = {}, {}
        ds = [None]
        prepared, last_page = {}, []

        def prepare(tile):
            if ds[0] is None:
                d, arrived = load_page(down_s.partition_broadcast(P), lambda pg: pg[:, :])
                dve.wait(arrived)
                t = dve.do(lambda e: nc.vector.tensor_scalar(page[d][:, :], page[d][:, :], sc[:, 5:6], None, ALU.mult), e_fin, D)
                ds[0] = (d, t)
            while not free_pages:
                yield BLOCKED
            d, d_ready = ds[0]
            i, before = take_page()
            arrived = load(page[i][:, :], x1_dram[tile], page_ev[i], sp, waits=(x1_stored[tile], *before))
            row = acc[:, tile, :]
            pool.wait(*acc_ready[tile, 0], *acc_ready[tile, 1], d_ready, pool_last[0])
            t = pool_last[0] = pool.do(lambda e: nc.gpsimd.tensor_tensor(row, row, page[d][:, :], ALU.mult), e_finpool, D)
            to_add.append((tile, i, t, arrived))
            if len(to_add) > 1:
                add_x1()

        to_add = []

        def add_x1():
            tile, i, t, arrived = to_add.pop(0)
            row = acc[:, tile, :]
            dve.wait(t, arrived)
            t = dve.do(lambda e: nc.vector.tensor_tensor(row, row, page[i][:, :], ALU.add), e_fin, D)
            give_page(i, t)
            prepared[tile] = t

        def finish(tile, r):
            y = last_page[tile % 2][0]
            row = acc[:, tile, :]
            dve.wait(r, prepared[tile])
            t = dve.do(lambda e: nc.vector.tensor_tensor(row, row, page[y][:, :], ALU.add), e_fin, D)
            last_page[tile % 2] = (y, (t,))

            def store(n):
                sp.wait(n)
                sp.do(lambda e: e.dma_start(out[tile], row), e_out, by=16)

            order.after([t], lambda: layernorm(row, tile % 2, t, store))

        e_finpool = ev("final_pool")
        e_out = ev("out_dma")
        NG = FC // GC

        def group_weights(g, kinds, last):
            for c in range(g * GC, min((g + 1) * GC, FC)):
                free = over
                if c >= NW:
                    while (c - NW) // GC not in last:
                        yield BLOCKED
                    free = (last[(c - NW) // GC],)
                yield from weights(c, kinds, free)

        def gate_up_weights(g):
            return group_weights(g, (0, 1), gu_last)

        def down_weights(g):
            return group_weights(g, (2,), down_last)

        def last_output():
            yield from output_stream
            retired.append(None)
            for i, tickets in [f for f in free_pages if f[0] >= KEPT]:
                free_pages.remove((i, tickets))
                give_page(i, *tickets)
            while len(retired) < 1 + NPAGE - KEPT:
                yield BLOCKED
            attention_over.extend([e_proj.so_far(), *[t for i in page_users for t in page_users[i]]])

        def ffn():
            while not projections_over:
                yield BLOCKED
            yield from gate_up_weights(0)
            loads = down_weights(0)
            pending = None
            for g in range(NG):
                for tb in range(B):
                    slot = (g * B + tb) % 2
                    ready = []
                    while tb not in x1T_ready or x1T_ready[tb][1] < NT * 16:
                        yield BLOCKED
                    downs = iter(())
                    for c in range(GC):
                        for said in gate_up(g, tb, slot, c, ready):
                            next(loads, None)
                            yield said
                        if pending and c == (pending[1] == 0):
                            if pending[1] == 0:
                                yield from loads
                                loads = gate_up_weights(pending[0] + 1)
                            while not attention_over:
                                yield BLOCKED
                            downs = down(*pending)
                        for said in itertools.islice(downs, DOWN_STEPS):
                            next(loads, None)
                            yield said
                    for said in downs:
                        next(loads, None)
                        yield said
                    pending = (g, tb, slot, ready)
                yield from loads
                loads = down_weights(g + 1)
            yield from down(*pending)

        NU = B * UNITS

        def attends():
            for u in range(NU):
                yield from attend(u)
            over.extend(e.so_far() for e in (e_proj, e_rope, e_ropep, e_nathi, e_natlo, e_tr, e_trc, e_v, e_hi, e_lo, e_smax,
                                             e_mx, e_mpart, e_mtr, e_mcopy, e_st, e_exp, e_causal, e_pv, e_den, *e_mrow))
            yield BLOCKED

        def all_maxima():
            for u in range(NU):
                yield from maxima(u)

        def projections():
            for u in range(NU):
                if u and u % UNITS == 0:
                    for k in range(0, KD, 2):
                        yield from load_x(u // UNITS, k)
                yield from project(u, u % UNITS == 0)
            projections_over.append(e_proj.so_far())

        def outputs():
            for b in range(B):
                yield from output(b)

        output_stream, x1T_stream, ffn_stream = outputs(), load_x1T(), ffn()
        order.run([attends(), first_loads(), all_maxima(), output_stream,
                   projections(), x1T_stream, ffn_stream], until=lambda: over)
        order.run([last_output(), ffn_stream, x1T_stream], by_progress=False)
        sp.wait(e_out.so_far())

        with nc.Block() as block:
            block.tensor(pe.run)
            block.scalar(act.run)
            block.vector(dve.run)
            block.gpsimd(pool.run)
            block.sync(sp.run)


def rope_tables():
    freqs = (np.float32(1.0) / np.float32(THETA) ** (np.arange(0, HD, 2, dtype=np.float32) / np.float32(HD))).astype(np.float32)
    ang = np.outer(np.arange(S, dtype=np.float32), freqs).astype(np.float32).astype(np.float64)
    cos, sin = np.cos(ang), np.sin(ang)
    c, s = np.concatenate([cos, cos], 1), np.concatenate([-sin, sin], 1)
    k = PROJ_DOWN * QK_UP
    q = k / np.sqrt(HD)
    t = np.stack([c * q, s * q, c * k, s * k], 1).astype(np.float32)
    return np.ascontiguousarray(t.reshape(NT, P, 4, HD).transpose(1, 0, 2, 3))


def causal_mask():
    i = np.arange(P)
    m = np.zeros((P, S), np.float32)
    m[:, S - P:] = np.where(i[None, :] > i[:, None], MASKED, 0.0)
    return m


def kernel(**inputs):
    import concourse.bacc as bacc
    from concourse.bass_utils import run_bass_kernel_spmd

    g = {k.replace("L0_", ""): np.asarray(v) for k, v in inputs.items()}
    bf16, f16 = mybir.dt.np(BF16), np.float16
    even_odd = np.concatenate([np.arange(0, HD, 2), np.arange(1, HD, 2)])

    def heads_split(w, n):
        return w.reshape(D, n, HD)[:, :, even_odd].reshape(D, n * HD)

    def chunked(w):
        return w.reshape(KD, P, -1).transpose(1, 0, 2)

    x = g["attn_x"]
    causal = causal_mask()
    arrays = {
        "xT": x.reshape(B, S, KD, P).transpose(0, 3, 2, 1),
        "x": x.reshape(TILES, P, D),
        "wq": chunked(heads_split(g["attn_wq"], NH)),
        "wkv": chunked(np.concatenate([heads_split(g["attn_wk"], NKV), g["attn_wv"]], 1)),
        "wo": chunked(g["attn_wo"]),
        "gateT": g["ffn_gate_t"].reshape(FC, P, KD, P).transpose(0, 3, 2, 1).reshape(FC, P, D),
        "upT": g["ffn_up_t"].reshape(FC, P, KD, P).transpose(0, 3, 2, 1).reshape(FC, P, D),
        "downT": g["ffn_down_t"].T.reshape(FC, P, D),
        "gate_s": g["ffn_gate_s"].reshape(FC, P).T,
        "up_s": g["ffn_up_s"].reshape(FC, P).T,
        "down_s": g["ffn_down_s"],
        "rope": rope_tables(),
        "causal": causal.astype(bf16),
        "identH": np.eye(P).astype(f16),
    }
    arrays = {k: np.ascontiguousarray(v) for k, v in arrays.items()}
    nc = bacc.Bacc("TRN2", target_bir_lowering=False, num_devices=1)
    args = {k: nc.dram_tensor(k, v.shape, mybir.dt.from_np(v.dtype), kind="ExternalInput").ap() for k, v in arrays.items()}
    out = nc.dram_tensor("out", [TILES, P, D], F32, kind="ExternalOutput").ap()
    block_kernel(nc, **args, out=out)
    got = run_bass_kernel_spmd(nc, [arrays], core_ids=[0]).results[0]["out"]
    return np.asarray(got).reshape(B, S, D)
```
